# Optimizing a Trainium2 kernel written in Bass

```python
import numpy as np
import jax
import jax.numpy as jnp

def _softmax(x, axis=-1):
    return jax.nn.softmax(x, axis=axis)

def _gelu(x):
    return jax.nn.gelu(x, approximate=True)

def _silu(x):
    return jax.nn.silu(x)

def _sigmoid(x):
    return jax.nn.sigmoid(x)

def _layernorm(x, axis=-1, eps=1e-05):
    m = jnp.mean(x, axis=axis, keepdims=True)
    v = jnp.var(x, axis=axis, keepdims=True)
    return (x - m) / jnp.sqrt(v + eps)

def _scatter_add(tgt, idx, src, axis=0):
    return tgt.at[idx].add(src)

def _segment_sum(src, seg, n):
    return jax.ops.segment_sum(src, seg, n)
kernel_name = 'mk_gnn_resnorm_d2_gnn_r8_6b898e'

def setup_inputs(seed: int=0):
    np.random.seed(seed)
    _w = jnp.asarray

    def _rec_inputs():
        import jax
        import jax.numpy as jnp
        _gk = jax.random.key(seed)
        x = -0.0003713 + 1 * jax.random.normal(jax.random.fold_in(_gk, 1), (6250, 128), jnp.float32)
        src = jax.random.randint(jax.random.fold_in(_gk, 2), (100000,), 0, 6250, jnp.int32)
        dst = jax.random.randint(jax.random.fold_in(_gk, 3), (100000,), 0, 6250, jnp.int32)
        _o = jnp.argsort(dst, stable=True)
        src = src[_o]
        dst = dst[_o]
        edge_attr_32 = 0.000189758 + 1.00013 * jax.random.normal(jax.random.fold_in(_gk, 11), (100000, 32), jnp.float32)
        return (x, src, dst, edge_attr_32)
    x, src, dst, edge_attr_32 = _rec_inputs()

    def _L0_gnn_setup():
        import jax, jax.numpy as jnp
        import numpy as np
        N_NODES = 12500
        N_EDGES = 200000
        IN_C = 128
        HID = 16
        OUT_C = 128

        def _sage_conv(x, src, dst, W, b, R):
            num_nodes = x.shape[0]
            agg = jax.ops.segment_sum(x[src], dst, num_segments=num_nodes)
            deg = jax.ops.segment_sum(jnp.ones_like(dst, x.dtype), dst, num_segments=num_nodes)
            mean = agg / jnp.maximum(deg, 1.0)[:, None]
            return mean @ W + b + x @ R
        key = jax.random.key(seed)
        ks = jax.random.split(key, 8)
        x = jax.random.normal(ks[0], (N_NODES, IN_C), dtype=jnp.float32)
        edge_index = jax.random.randint(ks[1], (2, N_EDGES), 0, N_NODES, dtype=jnp.int64)
        s1 = 1.0 / np.sqrt(IN_C)
        W1 = jax.random.uniform(ks[2], (IN_C, HID), jnp.float32, -s1, s1)
        b1 = jnp.zeros((HID,), jnp.float32)
        R1 = jax.random.uniform(ks[3], (IN_C, HID), jnp.float32, -s1, s1)
        s2 = 1.0 / np.sqrt(HID)
        W2 = jax.random.uniform(ks[4], (HID, OUT_C), jnp.float32, -s2, s2)
        b2 = jnp.zeros((OUT_C,), jnp.float32)
        R2 = jax.random.uniform(ks[5], (HID, OUT_C), jnp.float32, -s2, s2)
        return {'x': x, 'edge_index': edge_index, 'W1': W1, 'b1': b1, 'R1': R1, 'W2': W2, 'b2': b2, 'R2': R2}
    _L0_gnn_all = _L0_gnn_setup()
    _L0_gnn_in = {k: v for k, v in _L0_gnn_all.items() if k in ('W1', 'b1', 'R1', 'W2', 'b2', 'R2')}
    del _L0_gnn_all

    def _L1_gnn_setup():
        import jax, jax.numpy as jnp
        import numpy as np
        N_NODES = 12500
        N_EDGES = 200000
        IN_DIM = 128
        OUT_DIM = 128
        EDGE_DIM = 32
        EPS = 1e-05

        def _layernorm(h, gamma, beta):
            mu = jnp.mean(h, axis=-1, keepdims=True)
            var = jnp.var(h, axis=-1, keepdims=True)
            return (h - mu) * jax.lax.rsqrt(var + EPS) * gamma + beta
        key = jax.random.key(seed)
        ks = jax.random.split(key, 10)
        hid = OUT_DIM * 2
        x = jax.random.normal(ks[0], (N_NODES, IN_DIM), dtype=jnp.float32)
        edge_index = jax.random.randint(ks[1], (2, N_EDGES), 0, N_NODES, dtype=jnp.int64)
        edge_attr = jax.random.normal(ks[2], (N_EDGES, EDGE_DIM), dtype=jnp.float32)
        W1 = jax.random.normal(ks[3], (IN_DIM + EDGE_DIM, hid), dtype=jnp.float32) / np.sqrt(IN_DIM + EDGE_DIM)
        b1 = jnp.zeros((hid,), jnp.float32)
        g1 = jnp.ones((hid,), jnp.float32)
        be1 = jnp.zeros((hid,), jnp.float32)
        W2 = jax.random.normal(ks[4], (hid, OUT_DIM), dtype=jnp.float32) / np.sqrt(hid)
        b2 = jnp.zeros((OUT_DIM,), jnp.float32)
        Wu = jax.random.normal(ks[5], (IN_DIM + OUT_DIM, OUT_DIM), dtype=jnp.float32) / np.sqrt(IN_DIM + OUT_DIM)
        bu = jnp.zeros((OUT_DIM,), jnp.float32)
        gu = jnp.ones((OUT_DIM,), jnp.float32)
        beu = jnp.zeros((OUT_DIM,), jnp.float32)
        return {'x': x, 'edge_index': edge_index, 'edge_attr': edge_attr, 'W1': W1, 'b1': b1, 'g1': g1, 'be1': be1, 'W2': W2, 'b2': b2, 'Wu': Wu, 'bu': bu, 'gu': gu, 'beu': beu}
    _L1_gnn_all = _L1_gnn_setup()
    _L1_gnn_in = {k: v for k, v in _L1_gnn_all.items() if k in ('W1', 'b1', 'g1', 'be1', 'W2', 'b2', 'Wu', 'bu', 'gu', 'beu')}
    del _L1_gnn_all
    return {'x': x, 'src': src, 'dst': dst, 'edge_attr_32': edge_attr_32, 'L0_gnn_W1': _L0_gnn_in['W1'], 'L0_gnn_b1': _L0_gnn_in['b1'], 'L0_gnn_R1': _L0_gnn_in['R1'], 'L0_gnn_W2': _L0_gnn_in['W2'], 'L0_gnn_b2': _L0_gnn_in['b2'], 'L0_gnn_R2': _L0_gnn_in['R2'], 'L1_gnn_W1': _L1_gnn_in['W1'], 'L1_gnn_b1': _L1_gnn_in['b1'], 'L1_gnn_g1': _L1_gnn_in['g1'], 'L1_gnn_be1': _L1_gnn_in['be1'], 'L1_gnn_W2': _L1_gnn_in['W2'], 'L1_gnn_b2': _L1_gnn_in['b2'], 'L1_gnn_Wu': _L1_gnn_in['Wu'], 'L1_gnn_bu': _L1_gnn_in['bu'], 'L1_gnn_gu': _L1_gnn_in['gu'], 'L1_gnn_beu': _L1_gnn_in['beu']}

def reference(x, src, dst, edge_attr_32, L0_gnn_W1, L0_gnn_b1, L0_gnn_R1, L0_gnn_W2, L0_gnn_b2, L0_gnn_R2, L1_gnn_W1, L1_gnn_b1, L1_gnn_g1, L1_gnn_be1, L1_gnn_W2, L1_gnn_b2, L1_gnn_Wu, L1_gnn_bu, L1_gnn_gu, L1_gnn_beu):
    import jax
    import jax.numpy as jnp

    def _L0_gnn_ref(x, edge_index, W1, b1, R1, W2, b2, R2):
        import jax, jax.numpy as jnp
        import numpy as np
        N_NODES = 12500
        N_EDGES = 200000
        IN_C = 128
        HID = 16
        OUT_C = 128

        def _sage_conv(x, src, dst, W, b, R):
            num_nodes = x.shape[0]
            agg = jax.ops.segment_sum(x[src], dst, num_segments=num_nodes)
            deg = jax.ops.segment_sum(jnp.ones_like(dst, x.dtype), dst, num_segments=num_nodes)
            mean = agg / jnp.maximum(deg, 1.0)[:, None]
            return mean @ W + b + x @ R
        src, dst = (edge_index[0], edge_index[1])
        h = jax.nn.relu(_sage_conv(x, src, dst, W1, b1, R1))
        out = _sage_conv(h, src, dst, W2, b2, R2)
        return out

    def _L1_gnn_ref(x, edge_index, edge_attr, W1, b1, g1, be1, W2, b2, Wu, bu, gu, beu):
        import jax, jax.numpy as jnp
        import numpy as np
        N_NODES = 12500
        N_EDGES = 200000
        IN_DIM = 128
        OUT_DIM = 128
        EDGE_DIM = 32
        EPS = 1e-05

        def _layernorm(h, gamma, beta):
            mu = jnp.mean(h, axis=-1, keepdims=True)
            var = jnp.var(h, axis=-1, keepdims=True)
            return (h - mu) * jax.lax.rsqrt(var + EPS) * gamma + beta
        row, col = (edge_index[0], edge_index[1])
        msg_in = jnp.concatenate([x[row], edge_attr], axis=-1)
        h = msg_in @ W1 + b1
        h = jax.nn.gelu(_layernorm(h, g1, be1), approximate=False)
        msg = h @ W2 + b2
        agg = jax.ops.segment_sum(msg, col, num_segments=x.shape[0])
        u = jnp.concatenate([x, agg], axis=-1) @ Wu + bu
        u = jax.nn.gelu(_layernorm(u, gu, beu), approximate=False)
        return u + x
    edge_index = jnp.stack([src, dst])
    x = _layernorm(x + _L0_gnn_ref(x, edge_index, L0_gnn_W1, L0_gnn_b1, L0_gnn_R1, L0_gnn_W2, L0_gnn_b2, L0_gnn_R2), axis=-1)
    x = _layernorm(x + _L1_gnn_ref(x, edge_index, edge_attr_32, L1_gnn_W1, L1_gnn_b1, L1_gnn_g1, L1_gnn_be1, L1_gnn_W2, L1_gnn_b2, L1_gnn_Wu, L1_gnn_bu, L1_gnn_gu, L1_gnn_beu), axis=-1)
    return x

_drawn_inputs = setup_inputs


def setup_inputs(seed=0):
    import zlib

    import numpy as np

    out = dict(_drawn_inputs(seed))
    spreads = {'L0_gnn_b1': (0.0, 0.1),
     'L0_gnn_b2': (0.0, 0.1),
     'L1_gnn_b1': (0.0, 0.1),
     'L1_gnn_g1': (1.0, 0.2),
     'L1_gnn_be1': (0.0, 0.1),
     'L1_gnn_b2': (0.0, 0.1),
     'L1_gnn_bu': (0.0, 0.8),
     'L1_gnn_gu': (1.0, 0.2),
     'L1_gnn_beu': (0.0, 0.1)}
    factors = {}
    for name, (base, spread) in spreads.items():
        noise = np.random.default_rng([zlib.crc32(name.encode()), seed]).standard_normal(out[name].shape)
        drawn = base * np.exp(spread * noise) if base else spread * noise
        out[name] = jnp.asarray(drawn.astype(out[name].dtype))
    for name, factor in factors.items():
        out[name] = (out[name] * factor).astype(out[name].dtype)
    return out
```

```python
import concourse.bass as bass
from concourse import mybir
from contextlib import ExitStack

P = 128
G = 8
GE = G * P
WIN = 128
CH = 7
CN = CH * P
PARTS = 3


def gnn(nc, x, src, dst, ea, A, out):
    f32, bf16, i32 = mybir.dt.float32, mybir.dt.bfloat16, mybir.dt.int32
    ALU, ACT, AX = mybir.AluOpType, mybir.ActivationFunctionType, mybir.AxisListType

    N, C = x.shape
    E, EC = ea.shape
    H0 = A["L0_W1"].shape[1]
    H1 = A["L1_W1"].shape[1]
    HH = H1 // P
    NG = -(-E // GE)
    LAST = E - GE
    DOUBLE = ((NG - 1) * GE - LAST) // G
    NT = -(-N // P)
    NCH = NT // CH
    NP = NT * P
    TAIL = N - (NT - 1) * P
    TW = 64
    ONE = PARTS * H0
    QW = H1 + EC
    RW = QW + 1
    SUMW = NP + WIN
    EPS = 1e-5
    INVALID = 1.0e6
    assert NT % CH == 0 and NG % 2 == 0 and ((NG - 1) * GE - LAST) % G == 0

    edges = lambda a: a.rearrange("(p j) -> p j", j=G)
    src_of = lambda first: src[bass.ds(first, GE)].rearrange("(p j) -> p j", j=G)
    ea_of = lambda first: ea[bass.ds(first, GE), :].rearrange("(p j) c -> p (j c)", j=G)

    tab1 = nc.dram_tensor("tab_p", (NP, TW), bf16, kind="Internal").ap()
    tab2 = nc.dram_tensor("tab_h", (NP, TW), bf16, kind="Internal").ap()
    tab3 = nc.dram_tensor("tab_x1", (NP, RW), f32, kind="Internal").ap()

    ctx = ExitStack()
    with ctx:
        def sb(name, shape, dt=f32):
            return ctx.enter_context(nc.sbuf_tensor(name, shape, dt))

        def sem(name):
            return ctx.enter_context(nc.semaphore(name))

        sums = sb("sums", [P, HH, SUMW])
        x1s = sb("x1s", [P, NT, C])
        ux = sb("ux", [P, NT, C])
        xr = sb("xr", [P, NT, H0])
        hs = sb("hs", [P, NT, H0])
        deg = sb("deg", [P, NT])
        invdeg = sb("invdeg", [P, NT])
        rel0 = sb("rel0", [P, NG * G])
        rel = sb("rel", [P, NG * G])
        base0 = sb("base0", [1, NG], i32)
        base = sb("base", [1, NG], i32)
        turnsi = sb("turnsi", [1, 1], i32)
        ident = sb("ident", [P, P])
        iota = sb("iota", [P, WIN], bf16)
        S = sb("S", [TW, H0 + 1])
        WR1 = sb("WR1", [C, 2 * H0])
        WR2 = sb("WR2", [2 * H0 + 1, C])
        b1b = sb("b1b", [P, H0])
        WA = sb("WA", [C, QW + C])
        WAc = sb("WAc", [C, H1])
        WQ = sb("WQ", [P, QW])
        rowA = sb("rowA", [P, QW])
        b1c = sb("b1c", [P, H1])
        be1b = sb("be1b", [P, H1])
        bub, gub, beub = sb("bub", [P, C]), sb("gub", [P, C]), sb("beub", [P, C])
        W2Wu = sb("W2Wu", [P, HH, C])
        b2Wu = sb("b2Wu", [P, C])
        epsb = sb("epsb", [P, 1])
        idx = [sb(f"idx{u}", [P, G], i32) for u in range(2)]

        banks = [ctx.enter_context(nc.psum_tensor(f"bank{b}", [P, 512], f32)) for b in range(8)]

        with ExitStack() as tmp:
            def ts_(name, shape, dt=f32):
                return tmp.enter_context(nc.sbuf_tensor(name, shape, dt))

            dsti = ts_("dsti", [P, NG * G], i32)
            dstf = ts_("dstf", [P, NG * G])
            iotai = ts_("iotai", [P, WIN], i32)
            mins = ts_("mins", [P, NG])
            maxs = ts_("maxs", [P, NG])
            mm = ts_("mm", [NG, 2])
            basef = ts_("basef", [1, NG])
            spanf = ts_("spanf", [1, 1])
            ones = ts_("ones", [1, P])
            g1b = ts_("g1b", [P, H1])
            W1a = ts_("W1a", [C, H1])
            W1b = ts_("W1b", [P, H1])
            W2 = ts_("W2", [P, HH, C])
            Wub = ts_("Wub", [C, C])
            b2b = ts_("b2b", [P, C])
            stat = ts_("stat", [P, 4])
            tr = ts_("tr", [P, 9, P])
            tr2 = ts_("tr2", [P, HH, EC])
            s_dst, s_w, s_wc = sem("s_dst"), sem("s_w"), sem("s_wc")
            s_pool, s_id = sem("s_pool"), sem("s_id")
            s_v = sem("s_v")
            s_minmax, s_tmm, s_mm, s_row = sem("s_minmax"), sem("s_tmm"), sem("s_mm"), sem("s_row")
            s_rowsb, s_bb = sem("s_rowsb"), sem("s_bb")
            s_cent, s_tr, s_trsb, s_prod = sem("s_cent"), sem("s_tr"), sem("s_trsb"), sem("s_prod")
            s_two = sem("s_two")

            with nc.Block() as block:
                @block.sync
                def _(sp):
                    sp.dma_start(dsti[:, 0:(NG - 1) * G].rearrange("p (g j) -> p g j", j=G),
                                 dst[0:(NG - 1) * GE].rearrange("(g p j) -> p g j", p=P, j=G)).then_inc(s_dst, 16)
                    sp.dma_start(dsti[:, (NG - 1) * G:], edges(dst[LAST:E])).then_inc(s_dst, 16)
                    sp.dma_start(W1a[:], A["L1_W1"][0:C, :]).then_inc(s_w, 16)
                    for q in range(P // EC):
                        sp.dma_start(W1b[q * EC:(q + 1) * EC, :], A["L1_W1"][C:C + EC, :]).then_inc(s_w, 16)
                    sp.dma_start(W2[:], A["L1_W2"].rearrange("(h p) c -> p h c", p=P)).then_inc(s_w, 16)
                    sp.dma_start(Wub[:], A["L1_Wu"][C:2 * C, :]).then_inc(s_w, 16)
                    for to, name in ((g1b, "L1_g1"), (b1c, "L1_b1"), (b2b, "L1_b2")):
                        sp.dma_start(to[:], A[name][None, :].broadcast_to((P, to.shape[1]))).then_inc(s_w, 16)
                    sp.dma_start(WR1[:, 0:H0], A["L0_W1"]).then_inc(s_wc, 16)
                    sp.dma_start(WR1[:, H0:2 * H0], A["L0_R1"]).then_inc(s_wc, 16)
                    sp.dma_start(WR2[0:H0, :], A["L0_W2"]).then_inc(s_wc, 16)
                    sp.dma_start(WR2[H0:2 * H0, :], A["L0_R2"]).then_inc(s_wc, 16)
                    sp.dma_start(WR2[2 * H0:2 * H0 + 1, :], A["L0_b2"][None, :]).then_inc(s_wc, 16)
                    sp.dma_start(WA[:, QW:QW + C], A["L1_Wu"][0:C, :]).then_inc(s_wc, 16)
                    for to, name in ((b1b, "L0_b1"), (be1b, "L1_be1"), (bub, "L1_bu"), (gub, "L1_gu"),
                                     (beub, "L1_beu")):
                        sp.dma_start(to[:], A[name][None, :].broadcast_to((P, to.shape[1]))).then_inc(s_wc, 16)
                    sp.wait_ge(s_wc, 11 * 16)

                @block.gpsimd
                def _(pool):
                    nc.gpsimd.iota(iotai[:], [[1, WIN]], base=0, channel_multiplier=0)
                    nc.gpsimd.memset(ident[:], 0.0)
                    nc.gpsimd.memset(S[:], 0.0).then_inc(s_pool, 1)
                    pool.wait_ge(s_pool, 1)
                    nc.gpsimd.affine_select(out=ident[:], in_=ident[:], compare_op=ALU.not_equal, fill=1.0, base=0,
                                            pattern=[[-1, P]], channel_multiplier=1).then_inc(s_id, 1)
                    for k in range(PARTS):
                        nc.gpsimd.affine_select(out=S[:, 0:H0], in_=S[:, 0:H0], compare_op=ALU.not_equal,
                                                fill=1.0, base=-k * H0, pattern=[[-1, H0]],
                                                channel_multiplier=1).then_inc(s_pool, 1)
                        pool.wait_ge(s_pool, k + 2)
                    nc.gpsimd.affine_select(out=S[:, H0:H0 + 1], in_=S[:, H0:H0 + 1], compare_op=ALU.not_equal,
                                            fill=1.0, base=-ONE, pattern=[[-1, 1]],
                                            channel_multiplier=1).then_inc(s_pool, 1)

                @block.vector
                def _(v):
                    n = [0]

                    def link(ins):
                        n[0] += 1
                        ins.then_inc(s_v, 1)
                        v.wait_ge(s_v, n[0])

                    nc.vector.memset(epsb[:], EPS)
                    link(nc.vector.memset(ones[:], 1.0))
                    v.wait_ge(s_id, 1)
                    nc.vector.tensor_copy(iota[:], iotai[:])
                    v.wait_ge(s_dst, 32)
                    link(nc.vector.tensor_copy(dstf[:], dsti[:]))
                    view = dstf[:, :].rearrange("p (g j) -> p g j", j=G)
                    link(nc.vector.tensor_reduce(maxs[:], view, AX.X, ALU.max))
                    link(nc.vector.memset(dstf[0:DOUBLE, (NG - 1) * G:], INVALID))
                    nc.vector.tensor_reduce(mins[:], view, AX.X, ALU.min).then_inc(s_minmax, 1)
                    v.wait_ge(s_tmm, 1)
                    nc.vector.tensor_reduce(mm[:, 0:1], banks[0][0:NG, 0:P], AX.X, ALU.min)
                    link(nc.vector.tensor_reduce(mm[:, 1:2], banks[0][0:NG, P:2 * P], AX.X, ALU.max))
                    nc.vector.tensor_tensor(out=mm[:, 1:2], in0=mm[:, 1:2], in1=mm[:, 0:1],
                                            op=ALU.subtract).then_inc(s_mm, 1)
                    v.wait_ge(s_row, 1)
                    nc.vector.tensor_copy(basef[:], banks[1][0:1, 0:NG]).then_inc(s_rowsb, 1)
                    nc.vector.tensor_copy(base0[:], banks[1][0:1, 0:NG])
                    link(nc.vector.tensor_reduce(spanf[:], banks[1][0:1, P:P + NG], AX.X, ALU.max))
                    link(nc.vector.tensor_copy(turnsi[:], spanf[:]))
                    link(nc.vector.tensor_scalar(turnsi[:], turnsi[:], WIN.bit_length() - 1, None,
                                                 ALU.arith_shift_right))
                    nc.vector.tensor_scalar(turnsi[:], turnsi[:], 1, None, ALU.add)
                    v.wait_ge(s_bb, 1)
                    nc.vector.tensor_tensor(out=rel0[:, :].rearrange("p (g j) -> p g j", j=G), in0=view,
                                            in1=banks[2][:, 0:NG].unsqueeze(2).broadcast_to((P, NG, G)),
                                            op=ALU.subtract)
                    v.wait_ge(s_w, 16 * (3 + P // EC + 3))
                    for k, w in enumerate((W1a, W1b, b1c)):
                        nc.vector.tensor_reduce(stat[:, k:k + 1], w[:], AX.X, ALU.add)
                    link(nc.vector.memset(stat[:, 3:4], 0.0))
                    link(nc.vector.tensor_scalar(stat[:, 0:3], stat[:, 0:3], 1.0 / H1, None, ALU.mult))
                    nc.vector.tensor_scalar(WAc[:], W1a[:], stat[:, 0:1], None, ALU.subtract)
                    nc.vector.tensor_scalar(W1b[:], W1b[:], stat[:, 1:2], None, ALU.subtract)
                    link(nc.vector.tensor_scalar(b1c[:], b1c[:], stat[:, 2:3], None, ALU.subtract))
                    nc.vector.tensor_tensor(out=WA[:, 0:H1], in0=WAc[:], in1=g1b[:], op=ALU.mult)
                    nc.vector.tensor_tensor(out=WQ[:, 0:H1], in0=W1b[:], in1=g1b[:], op=ALU.mult)
                    nc.vector.tensor_tensor(out=rowA[:, 0:H1], in0=b1c[:], in1=g1b[:], op=ALU.mult).then_inc(s_cent, 1)
                    v.wait_ge(s_tr, 1)
                    for b in range(3):
                        k = min(4, 9 - 4 * b)
                        link(nc.vector.tensor_copy(tr[:, 4 * b:4 * b + k, :],
                                                   banks[3 + b][:, 0:k * P].rearrange("p (k c) -> p k c", c=P)))
                    nc.vector.tensor_scalar(tr2[:], tr[:, 2:2 + HH, 0:EC], 2.0, None, ALU.mult).then_inc(s_trsb, 1)
                    v.wait_ge(s_prod, 1)
                    nc.vector.tensor_copy(WA[:, H1:QW], banks[6][:, 0:EC])
                    nc.vector.tensor_copy(WQ[:, H1:QW], banks[6][:, EC:2 * EC])
                    nc.vector.tensor_copy(rowA[:, H1:QW], banks[6][:, 2 * EC:3 * EC])
                    nc.vector.tensor_copy(W2Wu[:], banks[7][:, 0:HH * C].rearrange("p (h c) -> p h c", c=C))
                    nc.vector.tensor_copy(b2Wu[:], banks[7][:, HH * C:(HH + 1) * C])

                @block.tensor
                def _(pe):
                    pe.wait_ge(s_id, 1)
                    pe.wait_ge(s_minmax, 1)
                    nc.tensor.transpose(banks[0][0:NG, 0:P], mins[:], ident[:])
                    nc.tensor.transpose(banks[0][0:NG, P:2 * P], maxs[:], ident[:]).then_inc(s_tmm, 1)
                    pe.wait_ge(s_mm, 1)
                    nc.tensor.matmul(banks[1][0:1, 0:NG], mm[:, 0:1], ident[0:NG, 0:NG], start=True, stop=True)
                    nc.tensor.matmul(banks[1][0:1, P:P + NG], mm[:, 1:2], ident[0:NG, 0:NG], start=True,
                                     stop=True).then_inc(s_row, 1)
                    pe.wait_ge(s_rowsb, 1)
                    nc.tensor.matmul(banks[2][:, 0:NG], ones[:], basef[:], start=True, stop=True).then_inc(s_bb, 1)
                    pe.wait_ge(s_cent, 1)
                    blocks = [w[:, h * P:(h + 1) * P] for w in (WAc, W1b, b1c) for h in range(HH)]
                    blocks += [W2[:, h, :] for h in range(HH)] + [b2b[:]]
                    for k, w in enumerate(blocks):
                        last = nc.tensor.transpose(banks[3 + k // 4][:, k % 4 * P:(k % 4 + 1) * P], w, ident[:])
                    last.then_inc(s_tr, 1)
                    pe.wait_ge(s_trsb, 1)
                    for h in range(HH):
                        nc.tensor.matmul(banks[6][:, 0:EC], tr[:, h, :], tr2[:, h, :], start=h == 0, stop=h == HH - 1)
                    for h in range(HH):
                        nc.tensor.matmul(banks[6][:, EC:2 * EC], tr[:, 2 + h, :], tr[:, 2 + h, 0:EC], start=h == 0,
                                         stop=h == HH - 1)
                    for h in range(HH):
                        nc.tensor.matmul(banks[6][:, 2 * EC:3 * EC], tr[:, 4 + h, :], tr2[:, h, :], start=h == 0,
                                         stop=h == HH - 1)
                    for h in range(HH):
                        nc.tensor.matmul(banks[7][:, h * C:(h + 1) * C], tr[:, 6 + h, :], Wub[:], start=True, stop=True)
                    nc.tensor.matmul(banks[7][:, HH * C:(HH + 1) * C], tr[:, 8, :], Wub[:], start=True,
                                     stop=True).then_inc(s_prod, 1)

        def chain(eng, s, start):
            n = [0]

            def link(ins):
                n[0] += 1
                ins.then_inc(s, 1)
                eng.wait_ge(s, start + n[0])
            return link, n

        SPLIT = 2 * PARTS - 2

        def split(link, tab, source, r):
            for k in range(PARTS - 1):
                part = tab[:, :, k * H0:(k + 1) * H0]
                link(nc.vector.tensor_copy(part, source))
                link(nc.vector.tensor_tensor(out=r[:], in0=source, in1=part, op=ALU.subtract))
                source = r[:]
            return nc.vector.tensor_copy(tab[:, :, (PARTS - 1) * H0:PARTS * H0], source)

        rows_of = lambda tab, i: tab[bass.ds(i * CN, CN), :].rearrange("(t p) c -> p t c", p=P)
        tiles = lambda bank, k, w: banks[bank][:, 0:k * w].rearrange("p (k c) -> p k c", c=w)

        def load_nodes(sp, to, i, s_loaded):
            sp.dma_start(to[:], rows_of(x, i)).then_inc(s_loaded, 16)

        def load_last_nodes(sp, to, s_tail, s_loaded):
            sp.dma_start(to[0:TAIL, CH - 1, :], x[N - TAIL:N, :]).then_inc(s_tail, 16)
            sp.wait_ge(s_tail, 16)
            first = (NCH - 1) * CN
            sp.dma_start(to[:, 0:CH - 1, :],
                         x[first:first + (CH - 1) * P, :].rearrange("(t p) c -> p t c", p=P)).then_inc(s_loaded, 16)

        with ExitStack() as tmp:
            xc = tmp.enter_context(nc.sbuf_tensor("n1_xc", [P, CH, C], f32))
            xT = tmp.enter_context(nc.sbuf_tensor("n1_xT", [P, CH, P], f32))
            tab = tmp.enter_context(nc.sbuf_tensor("n1_tab", [P, CH, TW], bf16))
            r = tmp.enter_context(nc.sbuf_tensor("n1_r", [P, CH, H0], f32))
            s_x, s_xt, s_xT, s_xTsb, s_p = sem("n1_x"), sem("n1_xt"), sem("n1_xT"), sem("n1_xTsb"), sem("n1_p")
            s_v, s_tab, s_st = sem("n1_v"), sem("n1_tab"), sem("n1_st")
            with nc.Block() as block:
                @block.sync
                def _(sp):
                    def store(i):
                        sp.wait_ge(s_tab, i + 1)
                        sp.dma_start(rows_of(tab1, i), tab[:]).then_inc(s_st, 16)

                    with sp.Fori(0, NCH - 1) as i:
                        sp.wait_ge(s_xT, i)
                        load_nodes(sp, xc, i, s_x)
                        store(i)
                    sp.wait_ge(s_xT, NCH - 1)
                    load_last_nodes(sp, xc, s_xt, s_x)
                    store(NCH - 1)
                    sp.wait_ge(s_st, 16 * NCH)

                @block.tensor
                def _(pe):
                    with pe.Fori(0, NCH) as i:
                        pe.wait_ge(s_x, 16 * i + 16)
                        pe.wait_ge(s_xTsb, i)
                        for k in range(CH):
                            last = nc.tensor.transpose(banks[k // 4][:, k % 4 * P:(k % 4 + 1) * P], xc[:, k, :], ident[:])
                        last.then_inc(s_xT, 1)
                        pe.wait_ge(s_xTsb, i + 1)
                        pe.wait_ge(s_tab, i)
                        for k in range(CH):
                            last = nc.tensor.matmul(banks[2][:, k * 2 * H0:(k + 1) * 2 * H0], xT[:, k, :], WR1[:],
                                                    start=True, stop=True)
                        last.then_inc(s_p, 1)

                @block.scalar
                def _(act):
                    with act.Fori(0, NCH) as i:
                        act.wait_ge(s_xT, i + 1)
                        act.wait_ge(s_p, i)
                        nc.scalar.copy(xT[:, 0:4, :], tiles(0, 4, P))
                        nc.scalar.copy(xT[:, 4:CH, :], tiles(1, CH - 4, P)).then_inc(s_xTsb, 1)

                @block.vector
                def _(v):
                    nc.vector.memset(tab[:], 0.0).then_inc(s_v, 1)
                    v.wait_ge(s_v, 1)
                    nc.vector.memset(tab[:, :, ONE:ONE + 1], 1.0)
                    with v.Fori(0, NCH) as i:
                        v.wait_ge(s_p, i + 1)
                        v.wait_ge(s_st, 16 * i)
                        ps = tiles(2, CH, 2 * H0)
                        nc.vector.tensor_tensor(out=xr[:, bass.ds(i * CH, CH), :], in0=ps[:, :, H0:2 * H0],
                                                in1=b1b[:, :].unsqueeze(1).broadcast_to((P, CH, H0)), op=ALU.add)
                        link, _ = chain(v, s_v, 1 + i * SPLIT)
                        split(link, tab, ps[:, :, 0:H0], r).then_inc(s_tab, 1)

        s_idx = [sem(f"a_idx{u}") for u in range(2)]
        s_rows = [sem(f"a_rows{u}") for u in range(2)]
        s_hot = sem("a_hot")
        s_sum = [sem(f"a_sum{u}") for u in range(2)]
        s_add = [sem(f"a_add{u}") for u in range(2)]
        s_ea = [sem(f"a_ea{u}") for u in range(2)]
        s_eaT, s_eaTsb, s_q, s_s = sem("a_eaT"), sem("a_eaTsb"), sem("a_q"), sem("a_s")
        s_var = [sem(f"a_var{u}") for u in range(2)]
        s_std, s_norm, s_act, s_c, s_rec = sem("a_std"), sem("a_norm"), sem("a_act"), sem("a_c"), sem("a_rec")
        of_pass = [*s_idx, s_hot, *s_sum, *s_add, *s_ea, s_eaT, s_eaTsb, s_q, s_s, *s_var, s_std,
                   s_norm, s_act, s_c, s_rec]

        def start_sums(halves, parts):
            with nc.Block() as block:
                @block.vector
                def _(v):
                    for h in halves:
                        nc.vector.memset(sums[0:parts, h, :], 0.0)
                    nc.vector.tensor_copy(rel[:], rel0[:])
                    nc.vector.tensor_copy(base[:], base0[:])

        def end_round():
            with nc.Block() as block:
                @block.gpsimd
                def _(pool):
                    pool.dma_reset(range(s_rows[0].num, s_rows[1].num + 1))
                    for s in s_rows:
                        pool.sem_clear(s)

                @block.vector
                def _(v):
                    for s in of_pass:
                        v.sem_clear(s)
                    nc.vector.tensor_scalar(rel[:], rel[:], float(WIN), None, ALU.subtract)
                    nc.vector.tensor_scalar(base[:], base[:], WIN, N, ALU.add, ALU.min)

        def load_indices(sp, i, u, last):
            sp.wait_ge(s_rows[u], 16 * G * i)
            sp.dma_start(idx[u][:], src_of(LAST if last else (2 * i + u) * GE)).then_inc(s_idx[u], 16)

        def gather(table, rows, u, w):
            nc.gpsimd.nop(nofuse=True)
            for j in range(G):
                nc.gpsimd.indirect_dma_start(
                    out=rows[u][:, j, :], out_offset=None, in_=table[:, :],
                    in_offset=bass.IndirectOffsetOnAxis(ap=idx[u][:, j:j + 1], axis=0)).then_inc(s_rows[u], 16)

        def one_hot(hot, g, u):
            for j in range(G):
                last = nc.vector.tensor_scalar(hot[u][:, j, :], iota[:], rel[:, bass.ds(g * G + j, 1)], None,
                                               ALU.is_equal)
            last.then_inc(s_hot, 1)

        def sum_pass0(table, half, rows, hot):
            with nc.Block() as block:
                @block.sync
                def _(sp):
                    with sp.Fori(0, NG // 2 - 1) as i:
                        for u in range(2):
                            load_indices(sp, i, u, False)
                    load_indices(sp, NG // 2 - 1, 0, False)
                    load_indices(sp, NG // 2 - 1, 1, True)

                @block.gpsimd
                def _(pool):
                    with pool.Fori(0, NG // 2) as i:
                        for u in range(2):
                            pool.wait_ge(s_idx[u], 16 * i + 16)
                            pool.wait_ge(s_sum[u], i)
                            gather(table, rows, u, TW)

                @block.vector
                def _(v):
                    with v.Fori(0, NG // 2) as i:
                        for u in range(2):
                            v.wait_ge(s_sum[u], i)
                            one_hot(hot, 2 * i + u, u)
                        for u in range(2):
                            at = v.value_load(base[0:1, bass.ds(2 * i + u, 1)], min_val=0, max_val=N)
                            v.wait_ge(s_sum[u], i + 1)
                            v.wait_ge(s_add[1 - u], i + u)
                            to = sums[0:TW, half, bass.ds(at, WIN)]
                            nc.vector.tensor_tensor(out=to, in0=to, in1=banks[u][0:TW, 0:WIN],
                                                    op=ALU.add).then_inc(s_add[u], 1)

                @block.tensor
                def _(pe):
                    with pe.Fori(0, NG // 2) as i:
                        for u in range(2):
                            pe.wait_ge(s_hot, 2 * i + u + 1)
                            pe.wait_ge(s_add[u], i)
                            pe.wait_ge(s_rows[u], 16 * G * i + 16 * G)
                            for j in range(G):
                                last = nc.tensor.matmul(banks[u][0:TW, 0:WIN], rows[u][:, j, :],
                                                        hot[u][:, j, :], start=j == 0, stop=j == G - 1)
                            last.then_inc(s_sum[u], 1)

        def rounds(one_round):
            turns = nc.values_load(turnsi[0:1, 0:1], min_val=1, max_val=-(-N // WIN))
            with nc.Fori(0, turns):
                one_round()
                end_round()

        def hidden_stage():
            with ExitStack() as tmp:
                sc = tmp.enter_context(nc.sbuf_tensor("n2_sc", [TW, CN], f32))
                tab = tmp.enter_context(nc.sbuf_tensor("n2_tab", [P, CH, TW], bf16))
                r = tmp.enter_context(nc.sbuf_tensor("n2_r", [P, CH, H0], f32))
                h = tmp.enter_context(nc.sbuf_tensor("n2_h", [P, CH, H0], f32))
                inv = tmp.enter_context(nc.sbuf_tensor("n2_inv", [P, CH], f32))
                s_sc, s_m, s_v, s_tab, s_st = sem("n2_sc"), sem("n2_m"), sem("n2_v"), sem("n2_tab"), sem("n2_st")
                with nc.Block() as block:
                    @block.sync
                    def _(sp):
                        with sp.Fori(0, NCH) as i:
                            sp.wait_ge(s_tab, i + 1)
                            sp.dma_start(rows_of(tab2, i), tab[:]).then_inc(s_st, 16)
                        sp.wait_ge(s_st, 16 * NCH)

                    @block.scalar
                    def _(act):
                        with act.Fori(0, NCH) as i:
                            act.wait_ge(s_m, i)
                            nc.scalar.copy(sc[:], sums[0:TW, 0, bass.ds(i * CN, CN)]).then_inc(s_sc, 1)

                    @block.tensor
                    def _(pe):
                        with pe.Fori(0, NCH) as i:
                            pe.wait_ge(s_sc, i + 1)
                            pe.wait_ge(s_tab, i)
                            for k in range(CH):
                                last = nc.tensor.matmul(banks[2][:, k * 32:k * 32 + H0 + 1], sc[:, k * P:(k + 1) * P],
                                                        S[:], start=True, stop=True)
                            last.then_inc(s_m, 1)

                    @block.vector
                    def _(v):
                        nc.vector.memset(tab[:], 0.0).then_inc(s_v, 1)
                        v.wait_ge(s_v, 1)
                        nc.vector.memset(tab[:, :, ONE:ONE + 1], 1.0)
                        steps = 6 + SPLIT
                        with v.Fori(0, NCH) as i:
                            v.wait_ge(s_m, i + 1)
                            ps = tiles(2, CH, 32)
                            at = bass.ds(i * CH, CH)

                            link, n = chain(v, s_v, 1 + i * steps)
                            nc.vector.tensor_copy(deg[:, at], ps[:, :, H0])
                            link(nc.vector.tensor_scalar(inv[:], ps[:, :, H0], 1.0, None, ALU.max))
                            link(nc.vector.reciprocal(inv[:], inv[:]))
                            nc.vector.tensor_copy(invdeg[:, at], inv[:])
                            link(nc.vector.tensor_tensor(out=h[:], in0=ps[:, :, 0:H0],
                                                         in1=inv[:, :].unsqueeze(2).broadcast_to((P, CH, H0)),
                                                         op=ALU.mult))
                            link(nc.vector.tensor_tensor(out=h[:], in0=h[:], in1=xr[:, at, :], op=ALU.add))
                            link(nc.vector.tensor_scalar(h[:], h[:], 0.0, None, ALU.max))
                            link(nc.vector.tensor_copy(hs[:, at, :], h[:]))
                            v.wait_ge(s_st, 16 * i)
                            split(link, tab, h[:], r).then_inc(s_tab, 1)
                            assert n[0] == steps

        def x1_stage():
            with ExitStack() as tmp:
                def t(name, shape, dt=f32):
                    return tmp.enter_context(nc.sbuf_tensor("n3_" + name, shape, dt))

                sc, xc, z = t("sc", [TW, CN]), t("xc", [P, CH, C]), t("z", [P, CH, 2 * H0])
                zT = t("zT", [2 * H0 + 1, CH, P])
                u1, st, ag = t("u", [P, CH, C]), t("st", [P, CH, 6]), t("ag", [P, CH, 2])
                std, x1c, x1T = t("std", [P, CH]), t("x1c", [P, CH, C]), t("x1T", [P, CH, P])
                tab, pc, junk = t("tab", [P, CH, RW]), t("pc", [P, H1]), t("junk", [P, H1])
                uxc, degc, sq = t("uxc", [P, C]), t("degc", [P, CH]), t("sq", [P, 1])
                s_sc, s_x, s_xt, s_m, s_z, s_zT, s_zTsb = (sem("n3_" + a) for a in "sc x xt m z zT zTsb".split())
                s_u, s_v, s_var, s_std, s_x1, s_x1T, s_x1Tsb = (
                    sem("n3_" + a) for a in "u v var std x1 x1T x1Tsb".split())
                s_wa, s_ev, s_st = (sem("n3_" + a) for a in "wa ev st".split())
                with nc.Block() as block:
                    @block.sync
                    def _(sp):
                        def store(i):
                            sp.wait_ge(s_ev, CH * (i + 1))
                            sp.dma_start(rows_of(tab3, i), tab[:]).then_inc(s_st, 16)

                        with sp.Fori(0, NCH - 1) as i:
                            sp.wait_ge(s_x1, i)
                            load_nodes(sp, xc, i, s_x)
                            store(i)
                        sp.wait_ge(s_x1, NCH - 1)
                        load_last_nodes(sp, xc, s_xt, s_x)
                        store(NCH - 1)
                        sp.wait_ge(s_st, 16 * NCH)

                    @block.scalar
                    def _(act):
                        with act.Fori(0, NCH) as i:
                            act.wait_ge(s_m, i)
                            nc.scalar.copy(sc[:], sums[0:TW, 1, bass.ds(i * CN, CN)]).then_inc(s_sc, 1)
                            act.wait_ge(s_zT, i + 1)
                            nc.scalar.copy(zT[0:2 * H0, 0:4, :], tiles(0, 4, P)[0:2 * H0])
                            nc.scalar.copy(zT[0:2 * H0, 4:CH, :], tiles(1, CH - 4, P)[0:2 * H0]).then_inc(s_zTsb, 1)
                            act.wait_ge(s_var, i + 1)
                            nc.scalar.activation(std[:], ag[:, :, 1], ACT.Sqrt, bias=epsb[:]).then_inc(s_std, 1)
                            act.wait_ge(s_x1T, i + 1)
                            nc.scalar.copy(x1T[:, 0:4, :], tiles(0, 4, P))
                            nc.scalar.copy(x1T[:, 4:CH, :], tiles(1, CH - 4, P)).then_inc(s_x1Tsb, 1)

                    @block.tensor
                    def _(pe):
                        with pe.Fori(0, NCH) as i:
                            pe.wait_ge(s_sc, i + 1)
                            pe.wait_ge(s_ev, CH * i)
                            for k in range(CH):
                                last = nc.tensor.matmul(banks[2][:, k * H0:(k + 1) * H0], sc[:, k * P:(k + 1) * P],
                                                        S[:, 0:H0], start=True, stop=True)
                            last.then_inc(s_m, 1)
                            pe.wait_ge(s_z, i + 1)
                            for k in range(CH):
                                last = nc.tensor.transpose(banks[k // 4][0:2 * H0, k % 4 * P:(k % 4 + 1) * P],
                                                           z[:, k, :], ident[:])
                            last.then_inc(s_zT, 1)
                            pe.wait_ge(s_zTsb, i + 1)
                            for k in range(CH):
                                last = nc.tensor.matmul(banks[3 + k // 4][:, k % 4 * C:(k % 4 + 1) * C], zT[:, k, :],
                                                        WR2[:], start=True, stop=True)
                            last.then_inc(s_u, 1)
                            pe.wait_ge(s_x1, i + 1)
                            for k in range(CH):
                                last = nc.tensor.transpose(banks[k // 4][:, k % 4 * P:(k % 4 + 1) * P], x1c[:, k, :],
                                                           ident[:])
                            last.then_inc(s_x1T, 1)
                            pe.wait_ge(s_x1Tsb, i + 1)
                            for k in range(CH):
                                if k >= 2:
                                    pe.wait_ge(s_ev, i * CH + k - 1)
                                nc.tensor.matmul(banks[5 + k % 2][:, 0:QW + C], x1T[:, k, :], WA[:], start=True,
                                                 stop=True)
                                b = (7, 2)[k % 2]
                                nc.tensor.matmul(banks[b][:, 0:H1], x1T[:, k, :], WAc[:], start=True,
                                                 stop=True).then_inc(s_wa, 1)

                    @block.vector
                    def _(v):
                        nc.vector.memset(zT[2 * H0:2 * H0 + 1, :, :], 1.0)
                        steps = 3 + 3 * CH
                        with v.Fori(0, NCH) as i:
                            link, n = chain(v, s_v, i * steps)
                            at = bass.ds(i * CH, CH)
                            v.wait_ge(s_m, i + 1)
                            nc.vector.tensor_copy(z[:, :, H0:2 * H0], hs[:, at, :])
                            nc.vector.tensor_copy(degc[:], deg[:, at])
                            nc.vector.tensor_tensor(out=z[:, :, 0:H0], in0=tiles(2, CH, H0),
                                                    in1=invdeg[:, at].unsqueeze(2).broadcast_to((P, CH, H0)),
                                                    op=ALU.mult).then_inc(s_z, 1)
                            v.wait_ge(s_u, i + 1)
                            v.wait_ge(s_x, 16 * i + 16)
                            nc.vector.tensor_tensor(out=u1[:, 0:4, :], in0=tiles(3, 4, C), in1=xc[:, 0:4, :], op=ALU.add)
                            link(nc.vector.tensor_tensor(out=u1[:, 4:CH, :], in0=tiles(4, CH - 4, C),
                                                         in1=xc[:, 4:CH, :], op=ALU.add))
                            moments(link, u1, st, ag, s_var)
                            v.wait_ge(s_std, i + 1)
                            link(nc.vector.reciprocal(std[:], std[:]))
                            normalize(x1c, u1, ag, std).then_inc(s_x1, 1)
                            v.wait_ge(s_x1, i + 1)
                            nc.vector.tensor_copy(x1s[:, at, :], x1c[:])
                            v.wait_ge(s_st, 16 * i)
                            for k in range(CH):
                                v.wait_ge(s_wa, i * CH + k + 1)
                                by_gamma, plain = banks[5 + k % 2], banks[(7, 2)[k % 2]]
                                nc.vector.tensor_tensor(out=tab[:, k, 0:QW], in0=by_gamma[:, 0:QW], in1=rowA[:],
                                                        op=ALU.add)
                                nc.vector.tensor_tensor(out=pc[:], in0=plain[:, 0:H1], in1=b1c[:], op=ALU.add)
                                link(nc.vector.scalar_tensor_tensor(out=uxc[:], in0=b2Wu[:], scalar=degc[:, k:k + 1],
                                                                    in1=bub[:], op0=ALU.mult, op1=ALU.add))
                                nc.vector.tensor_tensor(out=ux[:, bass.ds(i * CH + k, 1), :],
                                                        in0=by_gamma[:, QW:QW + C].unsqueeze(1),
                                                        in1=uxc[:, :].unsqueeze(1), op=ALU.add)
                                link(nc.vector.tensor_tensor(out=junk[:], in0=pc[:], in1=pc[:], op=ALU.mult))
                                link(nc.vector.tensor_reduce(sq[:], junk[:], AX.X, ALU.add))
                                nc.vector.tensor_copy(tab[:, k, QW:RW], sq[:]).then_inc(s_ev, 1)
                            assert n[0] == steps, n

        def moments(link, u, st, ag, s_done):
            for k in range(CH):
                last = nc.vector.bn_stats(st[:, k, :], u[:, k, :])
            link(last)
            nc.vector.nop(nofuse=True)
            for k in range(CH):
                last = nc.vector.bn_aggr(ag[:, k, :], st[:, k, :])
            last.then_inc(s_done, 1)

        def normalize(to, u, ag, rstd):
            for k in range(CH):
                last = nc.vector.tensor_scalar(to[:, k, :], u[:, k, :], ag[:, k, 0:1], rstd[:, k:k + 1],
                                               ALU.subtract, ALU.mult)
            return last

        def sum_pass1(rows, ebuf, eaT, s, hid, hot, prod, var, std, rstd):
            QB, TB, AB = range(4), 4, (5, 6)

            with nc.Block() as block:
                @block.sync
                def _(sp):
                    def load(i, u, last):
                        load_indices(sp, i, u, last)
                        sp.wait_ge(s_var[u], i)
                        sp.dma_start(ebuf[u][:], ea_of(LAST if last else (2 * i + u) * GE)).then_inc(s_ea[u], 16)

                    with sp.Fori(0, NG // 2 - 1) as i:
                        for u in range(2):
                            load(i, u, False)
                    load(NG // 2 - 1, 0, False)
                    load(NG // 2 - 1, 1, True)

                @block.gpsimd
                def _(pool):
                    with pool.Fori(0, NG // 2) as i:
                        for u in range(2):
                            pool.wait_ge(s_idx[u], 16 * i + 16)
                            pool.wait_ge(s_var[u], i)
                            gather(tab3, rows, u, RW)

                def turn_edges(pe, k, u):
                    g = 2 * k + u
                    pe.wait_ge(s_ea[u], 16 * k + 16)
                    pe.wait_ge(s_eaTsb, g)
                    for h in range(2):
                        last = nc.tensor.transpose(banks[TB][:, h * P:(h + 1) * P], ebuf[u][:, h * P:(h + 1) * P],
                                                   ident[:])
                    last.then_inc(s_eaT, 1)

                def products(pe, k, u, first):
                    g = 2 * k + u
                    pe.wait_ge(s_eaTsb, g + 1)
                    for j in range(G):
                        if not (first and j < len(QB)):
                            pe.wait_ge(s_s, G * g + j - len(QB) + 1)
                        h, q = divmod(j, P // EC)
                        nc.tensor.matmul(banks[QB[j % len(QB)]][:, 0:QW], eaT[u][q * EC:(q + 1) * EC, h, :],
                                         WQ[q * EC:(q + 1) * EC, :], start=True, stop=True).then_inc(s_q, 1)

                def sum_group(pe, k, u):
                    g = 2 * k + u
                    pe.wait_ge(s_act, 2 * g + 2)
                    pe.wait_ge(s_hot, g + 1)
                    pe.wait_ge(s_add[u], k)
                    for h in range(HH):
                        for j in range(G):
                            last = nc.tensor.matmul(banks[AB[u]][:, h * WIN:(h + 1) * WIN],
                                                    hid[u][:, j, h * P:(h + 1) * P], hot[u][:, j, :],
                                                    start=j == 0, stop=j == G - 1)
                    last.then_inc(s_sum[u], 1)

                @block.tensor
                def _(pe):
                    turn_edges(pe, 0, 0)
                    for k, u in ((0, 0), (0, 1)):
                        products(pe, k, u, k == u)
                        turn_edges(pe, k + u, 1 - u)
                    with pe.Fori(1, NG // 2 - 1) as k:
                        for u in range(2):
                            products(pe, k, u, False)
                            turn_edges(pe, k + u, 1 - u)
                            sum_group(pe, k - 1, u)
                    k = NG // 2 - 1
                    products(pe, k, 0, False)
                    turn_edges(pe, k, 1)
                    sum_group(pe, k - 1, 0)
                    products(pe, k, 1, False)
                    sum_group(pe, k - 1, 1)
                    sum_group(pe, k, 0)
                    sum_group(pe, k, 1)

                def keep_turned(act, k, u):
                    g = 2 * k + u
                    act.wait_ge(s_eaT, g + 1)
                    nc.scalar.copy(eaT[u][:], banks[TB][:, 0:2 * P].rearrange("p (h c) -> p h c", c=P)
                                   ).then_inc(s_eaTsb, 1)

                def deviation(act, k, u):
                    act.wait_ge(s_var[u], k + 1)
                    nc.scalar.activation(std[u][:], var[u][:], ACT.Sqrt, bias=epsb[:], scale=1.0 / H1
                                         ).then_inc(s_std, 1)

                def gelu(act, k, u):
                    g = 2 * k + u
                    for b in range(2):
                        act.wait_ge(s_norm, 2 * g + b + 1)
                        part = hid[u][:, b * G // 2:(b + 1) * G // 2, :]
                        nc.scalar.activation(part, part, ACT.Gelu).then_inc(s_act, 1)

                @block.scalar
                def _(act):
                    keep_turned(act, 0, 0)
                    deviation(act, 0, 0)
                    keep_turned(act, 0, 1)
                    deviation(act, 0, 1)
                    keep_turned(act, 1, 0)
                    gelu(act, 0, 0)
                    with act.Fori(1, NG // 2 - 1) as k:
                        for u in range(2):
                            deviation(act, k, u)
                            keep_turned(act, k + u, 1 - u)
                            gelu(act, k - 1 + u, 1 - u)
                    k = NG // 2 - 1
                    deviation(act, k, 0)
                    keep_turned(act, k, 1)
                    gelu(act, k - 1, 1)
                    deviation(act, k, 1)
                    gelu(act, k, 0)
                    gelu(act, k, 1)

                def add_rows(v, k, u, first=False):
                    g = 2 * k + u
                    if not first:
                        v.wait_ge(s_norm, 2 * g - 2)
                    v.wait_ge(s_rows[u], 16 * G * k + 16 * G)
                    for j in range(G):
                        v.wait_ge(s_q, G * g + j + 1)
                        nc.vector.tensor_tensor(out=s[u][:, j, :], in0=rows[u][:, j, 0:QW],
                                                in1=banks[QB[j % len(QB)]][:, 0:QW], op=ALU.add).then_inc(s_s, 1)
                    v.wait_ge(s_s, G * g + G)
                    v.wait_ge(s_ea[u], 16 * k + 16)
                    link, _ = chain(v, s_c, 3 * g)
                    link(nc.vector.tensor_tensor(out=prod[:], in0=s[u][:, :, H1:QW],
                                                 in1=ebuf[u][:, :].rearrange("p (j c) -> p j c", c=EC), op=ALU.mult))
                    link(nc.vector.tensor_reduce(var[u][:], prod[:], AX.X, ALU.add))
                    link(nc.vector.tensor_tensor(out=var[u][:], in0=var[u][:], in1=rows[u][:, :, QW], op=ALU.add))
                    nc.vector.tensor_scalar(var[u][:], var[u][:], 0.0, None, ALU.max).then_inc(s_var[u], 1)

                def scale_rows(v, k, u):
                    g = 2 * k + u
                    v.wait_ge(s_std, g + 1)
                    v.wait_ge(s_norm, 2 * g)
                    nc.vector.reciprocal(rstd[:], std[u][:]).then_inc(s_rec, 1)
                    v.wait_ge(s_rec, g + 1)
                    for j in range(G):
                        last = nc.vector.scalar_tensor_tensor(out=hid[u][:, j, :], in0=s[u][:, j, 0:H1],
                                                              scalar=rstd[:, j:j + 1], in1=be1b[:], op0=ALU.mult,
                                                              op1=ALU.add)
                        if j % 4 == 3:
                            last.then_inc(s_norm, 1)
                    one_hot(hot, g, u)

                def add_sums(v, k, u):
                    g = 2 * k + u
                    at = v.value_load(base[0:1, bass.ds(g, 1)], min_val=0, max_val=N)
                    v.wait_ge(s_sum[u], k + 1)
                    v.wait_ge(s_add[1 - u], k + u)
                    to = sums[:, :, bass.ds(at, WIN)]
                    nc.vector.tensor_tensor(out=to, in0=to, in1=banks[AB[u]][:, 0:HH * WIN].rearrange(
                        "p (h n) -> p h n", h=HH), op=ALU.add).then_inc(s_add[u], 1)

                @block.vector
                def _(v):
                    add_rows(v, 0, 0, True)
                    add_rows(v, 0, 1, True)
                    scale_rows(v, 0, 0)
                    with v.Fori(1, NG // 2) as k:
                        for u in range(2):
                            add_rows(v, k, u)
                            scale_rows(v, k - 1 + u, 1 - u)
                            add_sums(v, k - 1, u)
                    k = NG // 2 - 1
                    scale_rows(v, k, 1)
                    add_sums(v, k, 0)
                    add_sums(v, k, 1)

        def update_stage():
            with ExitStack() as tmp:
                def t(name, shape, dt=f32):
                    return tmp.enter_context(nc.sbuf_tensor("n4_" + name, shape, dt))

                sc = t("sc", [P, HH, CN])
                u1, w, y = t("u", [P, CH, C]), t("w", [P, CH, C]), t("y", [P, CH, C])
                st, ag, std = t("st", [P, CH, 6]), t("ag", [P, CH, 2]), t("std", [P, CH])
                s_sc, s_m, s_v, s_var, s_std, s_g, s_gd, s_y, s_st, s_stt = (
                    sem("n4_" + a) for a in "sc m v var std g gd y st stt".split())
                with nc.Block() as block:
                    @block.sync
                    def _(sp):
                        with sp.Fori(0, NCH - 1) as i:
                            sp.wait_ge(s_y, i + 1)
                            sp.dma_start(rows_of(out, i), y[:]).then_inc(s_st, 16)
                        sp.wait_ge(s_y, NCH)
                        first = (NCH - 1) * CN
                        sp.dma_start(out[first:first + (CH - 1) * P, :].rearrange("(t p) c -> p t c", p=P),
                                     y[:, 0:CH - 1, :]).then_inc(s_st, 16)
                        sp.dma_start(out[N - TAIL:N, :], y[0:TAIL, CH - 1, :]).then_inc(s_stt, 16)
                        sp.wait_ge(s_st, 16 * NCH)
                        sp.wait_ge(s_stt, 16)

                    @block.scalar
                    def _(act):
                        with act.Fori(0, NCH) as i:
                            act.wait_ge(s_m, i)
                            nc.scalar.copy(sc[:], sums[:, :, bass.ds(i * CN, CN)]).then_inc(s_sc, 1)
                            for n in range(2):
                                act.wait_ge(s_var, 2 * i + n + 1)
                                nc.scalar.activation(std[:], ag[:, :, 1], ACT.Sqrt, bias=epsb[:]).then_inc(s_std, 1)
                                if n == 0:
                                    act.wait_ge(s_g, i + 1)
                                    nc.scalar.activation(w[:], w[:], ACT.Gelu).then_inc(s_gd, 1)

                    @block.tensor
                    def _(pe):
                        with pe.Fori(0, NCH) as i:
                            pe.wait_ge(s_sc, i + 1)
                            pe.wait_ge(s_y, i)
                            for k in range(CH):
                                for h in range(HH):
                                    last = nc.tensor.matmul(banks[k // 4][:, k % 4 * C:(k % 4 + 1) * C],
                                                            sc[:, h, k * P:(k + 1) * P], W2Wu[:, h, :],
                                                            start=h == 0, stop=h == HH - 1)
                            last.then_inc(s_m, 1)

                    @block.vector
                    def _(v):
                        steps = 9
                        with v.Fori(0, NCH) as i:
                            link, n = chain(v, s_v, i * steps)
                            v.wait_ge(s_m, i + 1)
                            nc.vector.tensor_tensor(out=u1[:, 0:4, :], in0=tiles(0, 4, C),
                                                    in1=ux[:, bass.ds(i * CH, 4), :], op=ALU.add)
                            link(nc.vector.tensor_tensor(out=u1[:, 4:CH, :], in0=tiles(1, CH - 4, C),
                                                         in1=ux[:, bass.ds(i * CH + 4, CH - 4), :], op=ALU.add))
                            moments(link, u1, st, ag, s_var)
                            v.wait_ge(s_std, 2 * i + 1)
                            link(nc.vector.reciprocal(std[:], std[:]))
                            link(normalize(w, u1, ag, std))
                            link(nc.vector.tensor_tensor(out=w[:], in0=w[:], op=ALU.mult,
                                                         in1=gub[:, :].unsqueeze(1).broadcast_to((P, CH, C))))
                            nc.vector.tensor_tensor(out=w[:], in0=w[:], in1=beub[:, :].unsqueeze(1).broadcast_to(
                                (P, CH, C)), op=ALU.add).then_inc(s_g, 1)
                            link(nc.vector.tensor_scalar(u1[:], x1s[:, bass.ds(i * CH, CH), :], 2.0, None, ALU.mult))
                            v.wait_ge(s_gd, i + 1)
                            link(nc.vector.tensor_tensor(out=u1[:], in0=u1[:], in1=w[:], op=ALU.add))
                            moments(link, u1, st, ag, s_var)
                            v.wait_ge(s_std, 2 * i + 2)
                            link(nc.vector.reciprocal(std[:], std[:]))
                            v.wait_ge(s_st, 16 * i)
                            normalize(y, u1, ag, std).then_inc(s_y, 1)
                            assert n[0] == steps, n

        with ExitStack() as tmp:
            rows = [tmp.enter_context(nc.sbuf_tensor(f"rows0_{u}", [P, G, TW], bf16)) for u in range(2)]
            hot = [tmp.enter_context(nc.sbuf_tensor(f"hot0_{u}", [P, G, WIN], bf16)) for u in range(2)]
            start_sums((0, 1), TW)
            rounds(lambda: sum_pass0(tab1, 0, rows, hot))
            hidden_stage()
            start_sums((), TW)
            rounds(lambda: sum_pass0(tab2, 1, rows, hot))
        x1_stage()
        start_sums((0, 1), P)
        with ExitStack() as tmp:
            def two(name, shape, dt=f32):
                return [tmp.enter_context(nc.sbuf_tensor(f"{name}{u}", shape, dt)) for u in range(2)]

            rows, ebuf, eaT = two("rows1_", [P, G, RW]), two("ebuf", [P, G * EC]), two("eaT", [P, 2, P])
            s, hid, hot = two("s", [P, G, QW]), two("hid", [P, G, H1]), two("hot1_", [P, G, WIN])
            var, std = two("var", [P, G]), two("std", [P, G])
            prod = tmp.enter_context(nc.sbuf_tensor("prod", [P, G, EC], f32))
            rstd = tmp.enter_context(nc.sbuf_tensor("rstd", [P, G], f32))
            rounds(lambda: sum_pass1(rows, ebuf, eaT, s, hid, hot, prod, var, std, rstd))
        update_stage()


_INS = ['x', 'src', 'dst', 'edge_attr_32', 'L0_gnn_W1', 'L0_gnn_b1', 'L0_gnn_R1', 'L0_gnn_W2', 'L0_gnn_b2', 'L0_gnn_R2',
        'L1_gnn_W1', 'L1_gnn_b1', 'L1_gnn_g1', 'L1_gnn_be1', 'L1_gnn_W2', 'L1_gnn_b2', 'L1_gnn_Wu', 'L1_gnn_bu',
        'L1_gnn_gu', 'L1_gnn_beu']


def kernel(**inputs):
    import numpy as _np
    import concourse.bacc as _bacc
    from concourse import mybir as _mybir
    from concourse.bass_utils import run_bass_kernel_spmd as _run

    nc = _bacc.Bacc("TRN2", target_bir_lowering=False, num_devices=1)
    arrays, args = {}, {}
    for name in _INS:
        a = _np.ascontiguousarray(inputs[name])
        arrays[f"in_{name}"] = a
        args[name] = nc.dram_tensor(f"in_{name}", a.shape, _mybir.dt.from_np(a.dtype), kind="ExternalInput").ap()
    out = nc.dram_tensor("out", args["x"].shape, _mybir.dt.float32, kind="ExternalOutput").ap()
    weights = {name.replace("_gnn", ""): args[name] for name in _INS[4:]}
    gnn(nc, args["x"], args["src"], args["dst"], args["edge_attr_32"], weights, out)
    r = _run(nc, [arrays], core_ids=[0])
    return r.results[0]["out"]
```

```python
import concourse.bass as bass
from concourse import mybir
from contextlib import ExitStack

P = 128
G = 8
GE = G * P
WIN = 128
CH = 7
CN = CH * P
W = 14
B = 9
PARTS = 3


def gnn(nc, x, src, dst, ea, A, out):
    f32, bf16, i32 = mybir.dt.float32, mybir.dt.bfloat16, mybir.dt.int32
    ALU, ACT, AX = mybir.AluOpType, mybir.ActivationFunctionType, mybir.AxisListType

    N, C = x.shape
    E, EC = ea.shape
    H0 = A["L0_W1"].shape[1]
    H1 = A["L1_W1"].shape[1]
    HH = H1 // P
    NG = -(-E // GE)
    LAST = E - GE
    DOUBLE = ((NG - 1) * GE - LAST) // G
    NT = -(-N // P)
    NCH = NT // CH
    NP = NT * P
    TAIL = N - (NT - 1) * P
    TW = 64
    ONE = PARTS * H0
    QW = H1 + EC
    RW = QW + 1
    SUMW = NP + WIN
    EPS = 1e-5
    INVALID = 1.0e6
    TC = ONE + 1

    NGA = 37
    EA = NGA * GE
    NCOL = -(-(E - EA) // P)
    DUP = NCOL * P - (E - EA)
    NB = NCOL // B
    BR = P // B * B
    NBLK = -(-NCOL // BR)
    HI = NT + NT % 2
    HB = HI // 2 * W
    LB = BR // B
    IT = 9
    assert NCOL % B == 0 and NB == 6 * IT and NGA == 4 * IT + 1 and NBLK * BR <= 512
    assert DUP < P and HB <= 512 and B * W <= P

    assert NT % CH == 0 and NG % 2 == 0 and ((NG - 1) * GE - LAST) % G == 0

    edges = lambda a: a.rearrange("(p j) -> p j", j=G)
    src_of = lambda first: src[bass.ds(first, GE)].rearrange("(p j) -> p j", j=G)
    ea_of = lambda first: ea[bass.ds(first, GE), :].rearrange("(p j) c -> p (j c)", j=G)

    tab1 = nc.dram_tensor("tab_p", (NP, TW), bf16, kind="Internal").ap()
    tab2 = nc.dram_tensor("tab_h", (NP, TW), bf16, kind="Internal").ap()
    tab3 = nc.dram_tensor("tab_x1", (NP, RW), f32, kind="Internal").ap()

    ctx = ExitStack()
    with ctx:
        def sb(name, shape, dt=f32):
            return ctx.enter_context(nc.sbuf_tensor(name, shape, dt))

        def sem(name):
            return ctx.enter_context(nc.semaphore(name))

        sums = sb("sums", [P, HH, SUMW])
        x1s = sb("x1s", [P, NT, C])
        ux = sb("ux", [P, NT, C])
        xr = sb("xr", [P, NT, H0])
        hs = sb("hs", [P, NT, H0])
        deg = sb("deg", [P, NT])
        invdeg = sb("invdeg", [P, NT])
        rel0 = sb("rel0", [P, NG * G])
        rel = sb("rel", [P, NG * G])
        base0 = sb("base0", [1, NG], i32)
        base = sb("base", [1, NG], i32)
        general = sb("general", [1, 1], i32)
        lo = sb("lo", [P, NBLK * BR])
        comp = sb("comp", [P, NBLK * BR])
        pos = sb("pos", [P, NBLK * LB])
        bbase = sb("bbase", [1, NBLK * LB], i32)
        wide = sb("wide", [P, 2 * HB], mybir.dt.float16)
        table = sb("table", [P, NT, TW], bf16)
        turnsi = sb("turnsi", [1, 1], i32)
        gspan = sb("gspan", [1, 1])
        ident = sb("ident", [P, P])
        iota = sb("iota", [P, WIN], bf16)
        S = sb("S", [TC, H0 + 1])
        WR1 = sb("WR1", [C, 2 * H0])
        WR2 = sb("WR2", [2 * H0 + 1, C])
        b1b = sb("b1b", [P, H0])
        WA = sb("WA", [C, QW + C])
        WAc = sb("WAc", [C, H1])
        WQ = sb("WQ", [P, QW])
        rowA = sb("rowA", [P, QW])
        b1c = sb("b1c", [P, H1])
        be1b = sb("be1b", [P, H1])
        bub, gub, beub = sb("bub", [P, C]), sb("gub", [P, C]), sb("beub", [P, C])
        W2Wu = sb("W2Wu", [P, HH, C])
        b2Wu = sb("b2Wu", [P, C])
        epsb = sb("epsb", [P, 1])
        idx = [sb(f"idx{u}", [P, G], i32) for u in range(2)]

        zbanks = [ctx.enter_context(nc.psum_tensor(f"banks{2 * b}", [P, 1024], f32)) for b in range(3)]
        banks = [zbanks[b // 2][:, b % 2 * 512:(b % 2 + 1) * 512] for b in range(6)]
        banks += [ctx.enter_context(nc.psum_tensor(f"bank{b}", [P, 512], f32)) for b in (6, 7)]

        with ExitStack() as tmp:
            def ts_(name, shape, dt=f32):
                return tmp.enter_context(nc.sbuf_tensor(name, shape, dt))

            dsti = ts_("dsti", [P, NG * G], i32)
            dstf = ts_("dstf", [P, NG * G])
            iotai = ts_("iotai", [P, 2 * HB], i32)
            mins = ts_("mins", [P, NG])
            maxs = ts_("maxs", [P, NG])
            mm = ts_("mm", [NG, 2])
            basef = ts_("basef", [1, NG])
            spanf = ts_("spanf", [1, 1])
            ones = ts_("ones", [1, P])
            g1b = ts_("g1b", [P, H1])
            W1a = ts_("W1a", [C, H1])
            W1b = ts_("W1b", [P, H1])
            W2 = ts_("W2", [P, HH, C])
            Wub = ts_("Wub", [C, C])
            b2b = ts_("b2b", [P, C])
            stat = ts_("stat", [P, 4])
            tr = ts_("tr", [P, 9, P])
            tr2 = ts_("tr2", [P, HH, EC])
            s_dst, s_w, s_wc = sem("s_dst"), sem("s_w"), sem("s_wc")
            s_pool, s_id = sem("s_pool"), sem("s_id")
            s_v = sem("s_v")
            s_minmax, s_tmm, s_mm, s_row = sem("s_minmax"), sem("s_tmm"), sem("s_mm"), sem("s_row")
            s_rowsb, s_bb = sem("s_rowsb"), sem("s_bb")
            s_cent, s_tr, s_trsb, s_prod = sem("s_cent"), sem("s_tr"), sem("s_trsb"), sem("s_prod")
            s_two = sem("s_two")

            with nc.Block() as block:
                @block.sync
                def _(sp):
                    sp.dma_start(dsti[:, 0:(NG - 1) * G].rearrange("p (g j) -> p g j", j=G),
                                 dst[0:(NG - 1) * GE].rearrange("(g p j) -> p g j", p=P, j=G)).then_inc(s_dst, 16)
                    sp.dma_start(dsti[:, (NG - 1) * G:], edges(dst[LAST:E])).then_inc(s_dst, 16)
                    sp.dma_start(W1a[:], A["L1_W1"][0:C, :]).then_inc(s_w, 16)
                    for q in range(P // EC):
                        sp.dma_start(W1b[q * EC:(q + 1) * EC, :], A["L1_W1"][C:C + EC, :]).then_inc(s_w, 16)
                    sp.dma_start(W2[:], A["L1_W2"].rearrange("(h p) c -> p h c", p=P)).then_inc(s_w, 16)
                    sp.dma_start(Wub[:], A["L1_Wu"][C:2 * C, :]).then_inc(s_w, 16)
                    for to, name in ((g1b, "L1_g1"), (b1c, "L1_b1"), (b2b, "L1_b2")):
                        sp.dma_start(to[:], A[name][None, :].broadcast_to((P, to.shape[1]))).then_inc(s_w, 16)
                    sp.dma_start(WR1[:, 0:H0], A["L0_W1"]).then_inc(s_wc, 16)
                    sp.dma_start(WR1[:, H0:2 * H0], A["L0_R1"]).then_inc(s_wc, 16)
                    sp.dma_start(WR2[0:H0, :], A["L0_W2"]).then_inc(s_wc, 16)
                    sp.dma_start(WR2[H0:2 * H0, :], A["L0_R2"]).then_inc(s_wc, 16)
                    sp.dma_start(WR2[2 * H0:2 * H0 + 1, :], A["L0_b2"][None, :]).then_inc(s_wc, 16)
                    sp.dma_start(WA[:, QW:QW + C], A["L1_Wu"][0:C, :]).then_inc(s_wc, 16)
                    for to, name in ((b1b, "L0_b1"), (be1b, "L1_be1"), (bub, "L1_bu"), (gub, "L1_gu"),
                                     (beub, "L1_beu")):
                        sp.dma_start(to[:], A[name][None, :].broadcast_to((P, to.shape[1]))).then_inc(s_wc, 16)
                    sp.wait_ge(s_wc, 11 * 16)

                @block.gpsimd
                def _(pool):
                    nc.gpsimd.iota(iotai[:], [[1, 2 * HB]], base=0, channel_multiplier=0)
                    nc.gpsimd.memset(ident[:], 0.0)
                    nc.gpsimd.memset(S[:], 0.0).then_inc(s_pool, 1)
                    pool.wait_ge(s_pool, 1)
                    nc.gpsimd.affine_select(out=ident[:], in_=ident[:], compare_op=ALU.not_equal, fill=1.0, base=0,
                                            pattern=[[-1, P]], channel_multiplier=1).then_inc(s_id, 1)
                    for k in range(PARTS):
                        nc.gpsimd.affine_select(out=S[:, 0:H0], in_=S[:, 0:H0], compare_op=ALU.not_equal,
                                                fill=1.0, base=-k * H0, pattern=[[-1, H0]],
                                                channel_multiplier=1).then_inc(s_pool, 1)
                        pool.wait_ge(s_pool, k + 2)
                    nc.gpsimd.affine_select(out=S[:, H0:H0 + 1], in_=S[:, H0:H0 + 1], compare_op=ALU.not_equal,
                                            fill=1.0, base=-ONE, pattern=[[-1, 1]],
                                            channel_multiplier=1).then_inc(s_pool, 1)

                @block.vector
                def _(v):
                    n = [0]

                    def link(ins):
                        n[0] += 1
                        ins.then_inc(s_v, 1)
                        v.wait_ge(s_v, n[0])

                    nc.vector.memset(epsb[:], EPS)
                    link(nc.vector.memset(ones[:], 1.0))
                    v.wait_ge(s_id, 1)
                    nc.vector.tensor_copy(iota[:], iotai[:, 0:WIN])
                    nc.vector.tensor_copy(wide[:], iotai[:])
                    v.wait_ge(s_dst, 32)
                    link(nc.vector.tensor_copy(dstf[:], dsti[:]))
                    view = dstf[:, :].rearrange("p (g j) -> p g j", j=G)
                    link(nc.vector.tensor_reduce(maxs[:], view, AX.X, ALU.max))
                    link(nc.vector.memset(dstf[0:DOUBLE, (NG - 1) * G:], INVALID))
                    nc.vector.tensor_reduce(mins[:], view, AX.X, ALU.min).then_inc(s_minmax, 1)
                    v.wait_ge(s_tmm, 1)
                    nc.vector.tensor_reduce(mm[:, 0:1], banks[0][0:NG, 0:P], AX.X, ALU.min)
                    link(nc.vector.tensor_reduce(mm[:, 1:2], banks[0][0:NG, P:2 * P], AX.X, ALU.max))
                    nc.vector.tensor_tensor(out=mm[:, 1:2], in0=mm[:, 1:2], in1=mm[:, 0:1],
                                            op=ALU.subtract).then_inc(s_mm, 1)
                    v.wait_ge(s_row, 1)
                    nc.vector.tensor_copy(basef[:], banks[1][0:1, 0:NG]).then_inc(s_rowsb, 1)
                    nc.vector.tensor_copy(base0[:], banks[1][0:1, 0:NG])
                    link(nc.vector.tensor_reduce(spanf[:], banks[1][0:1, P:P + NG], AX.X, ALU.max))
                    nc.vector.tensor_copy(gspan[:], spanf[:])
                    link(nc.vector.tensor_copy(turnsi[:], spanf[:]))
                    link(nc.vector.tensor_scalar(turnsi[:], turnsi[:], WIN.bit_length() - 1, None,
                                                 ALU.arith_shift_right))
                    nc.vector.tensor_scalar(turnsi[:], turnsi[:], 1, None, ALU.add)
                    v.wait_ge(s_bb, 1)
                    nc.vector.tensor_tensor(out=rel0[:, :].rearrange("p (g j) -> p g j", j=G), in0=view,
                                            in1=banks[2][:, 0:NG].unsqueeze(2).broadcast_to((P, NG, G)),
                                            op=ALU.subtract)
                    v.wait_ge(s_w, 16 * (3 + P // EC + 3))
                    for k, w in enumerate((W1a, W1b, b1c)):
                        nc.vector.tensor_reduce(stat[:, k:k + 1], w[:], AX.X, ALU.add)
                    link(nc.vector.memset(stat[:, 3:4], 0.0))
                    link(nc.vector.tensor_scalar(stat[:, 0:3], stat[:, 0:3], 1.0 / H1, None, ALU.mult))
                    nc.vector.tensor_scalar(WAc[:], W1a[:], stat[:, 0:1], None, ALU.subtract)
                    nc.vector.tensor_scalar(W1b[:], W1b[:], stat[:, 1:2], None, ALU.subtract)
                    link(nc.vector.tensor_scalar(b1c[:], b1c[:], stat[:, 2:3], None, ALU.subtract))
                    nc.vector.tensor_tensor(out=WA[:, 0:H1], in0=WAc[:], in1=g1b[:], op=ALU.mult)
                    nc.vector.tensor_tensor(out=WQ[:, 0:H1], in0=W1b[:], in1=g1b[:], op=ALU.mult)
                    nc.vector.tensor_tensor(out=rowA[:, 0:H1], in0=b1c[:], in1=g1b[:], op=ALU.mult).then_inc(s_cent, 1)
                    v.wait_ge(s_tr, 1)
                    for b in range(3):
                        k = min(4, 9 - 4 * b)
                        link(nc.vector.tensor_copy(tr[:, 4 * b:4 * b + k, :],
                                                   banks[3 + b][:, 0:k * P].rearrange("p (k c) -> p k c", c=P)))
                    nc.vector.tensor_scalar(tr2[:], tr[:, 2:2 + HH, 0:EC], 2.0, None, ALU.mult).then_inc(s_trsb, 1)
                    v.wait_ge(s_prod, 1)
                    nc.vector.tensor_copy(WA[:, H1:QW], banks[6][:, 0:EC])
                    nc.vector.tensor_copy(WQ[:, H1:QW], banks[6][:, EC:2 * EC])
                    nc.vector.tensor_copy(rowA[:, H1:QW], banks[6][:, 2 * EC:3 * EC])
                    nc.vector.tensor_copy(W2Wu[:], banks[7][:, 0:HH * C].rearrange("p (h c) -> p h c", c=C))
                    nc.vector.tensor_copy(b2Wu[:], banks[7][:, HH * C:(HH + 1) * C])

                @block.tensor
                def _(pe):
                    pe.wait_ge(s_id, 1)
                    pe.wait_ge(s_minmax, 1)
                    nc.tensor.transpose(banks[0][0:NG, 0:P], mins[:], ident[:])
                    nc.tensor.transpose(banks[0][0:NG, P:2 * P], maxs[:], ident[:]).then_inc(s_tmm, 1)
                    pe.wait_ge(s_mm, 1)
                    nc.tensor.matmul(banks[1][0:1, 0:NG], mm[:, 0:1], ident[0:NG, 0:NG], start=True, stop=True)
                    nc.tensor.matmul(banks[1][0:1, P:P + NG], mm[:, 1:2], ident[0:NG, 0:NG], start=True,
                                     stop=True).then_inc(s_row, 1)
                    pe.wait_ge(s_rowsb, 1)
                    nc.tensor.matmul(banks[2][:, 0:NG], ones[:], basef[:], start=True, stop=True).then_inc(s_bb, 1)
                    pe.wait_ge(s_cent, 1)
                    blocks = [w[:, h * P:(h + 1) * P] for w in (WAc, W1b, b1c) for h in range(HH)]
                    blocks += [W2[:, h, :] for h in range(HH)] + [b2b[:]]
                    for k, w in enumerate(blocks):
                        last = nc.tensor.transpose(banks[3 + k // 4][:, k % 4 * P:(k % 4 + 1) * P], w, ident[:])
                    last.then_inc(s_tr, 1)
                    pe.wait_ge(s_trsb, 1)
                    for h in range(HH):
                        nc.tensor.matmul(banks[6][:, 0:EC], tr[:, h, :], tr2[:, h, :], start=h == 0, stop=h == HH - 1)
                    for h in range(HH):
                        nc.tensor.matmul(banks[6][:, EC:2 * EC], tr[:, 2 + h, :], tr[:, 2 + h, 0:EC], start=h == 0,
                                         stop=h == HH - 1)
                    for h in range(HH):
                        nc.tensor.matmul(banks[6][:, 2 * EC:3 * EC], tr[:, 4 + h, :], tr2[:, h, :], start=h == 0,
                                         stop=h == HH - 1)
                    for h in range(HH):
                        nc.tensor.matmul(banks[7][:, h * C:(h + 1) * C], tr[:, 6 + h, :], Wub[:], start=True, stop=True)
                    nc.tensor.matmul(banks[7][:, HH * C:(HH + 1) * C], tr[:, 8, :], Wub[:], start=True,
                                     stop=True).then_inc(s_prod, 1)

        def need(eng, s, value):
            if not isinstance(value, int) or value > 0:
                eng.wait_ge(s, value)

        def each(eng, n, first=1):
            def run(body):
                for i in range(first):
                    body(i)
                with eng.Fori(first, n) as i:
                    body(i)
            return run

        def from_one(eng, n):
            def run(body):
                body(1)
                with eng.Fori(2, n) as k:
                    body(k)
            return run

        def chain(eng, s, start):
            n = [0]

            def link(ins):
                n[0] += 1
                ins.then_inc(s, 1)
                eng.wait_ge(s, start + n[0])
            return link, n

        SPLIT = 2 * PARTS - 2

        def split(link, tab, source, r):
            for k in range(PARTS - 1):
                part = tab[:, :, k * H0:(k + 1) * H0]
                link(nc.vector.tensor_copy(part, source))
                link(nc.vector.tensor_tensor(out=r[:], in0=source, in1=part, op=ALU.subtract))
                source = r[:]
            return nc.vector.tensor_copy(tab[:, :, (PARTS - 1) * H0:PARTS * H0], source)

        with ExitStack() as tmp:
            def ts2(name, shape, dt=f32):
                return tmp.enter_context(nc.sbuf_tensor("c_" + name, shape, dt))

            dcol, scol = ts2("dcol", [BR, NBLK, P], i32), ts2("scol", [BR, NBLK, P], i32)
            dcf, scf = ts2("dcf", [BR, NBLK, P]), ts2("scf", [BR, NBLK, P])
            cmm = ts2("cmm", [BR, 2, NBLK])
            rows_mm = ts2("rows", [1, 2, NBLK * BR])
            ones = ts2("ones", [1, P])
            startb = ts2("startb", [P, NBLK * BR])
            srcf, hi = ts2("srcf", [P, NBLK * BR]), ts2("hi", [P, NBLK * BR])
            srci, hii = ts2("srci", [P, NBLK * BR], i32), ts2("hii", [P, NBLK * BR], i32)
            ok = ts2("ok", [P, NBLK * BR])
            which = ts2("which", [BR, B, W])
            batch = ts2("batch", [BR, LB])
            starts = ts2("starts", [BR, NBLK, LB])
            within = ts2("within", [P, 1])
            bb = ts2("bb", [P, NBLK * LB])
            bs = ts2("bs", [1, NBLK * LB])
            bad = ts2("bad", [1, 4])
            s_col, s_pool, s_v = sem("c_col"), sem("c_pool"), sem("c_v")
            s_mm, s_rows_, s_rowsb, s_st, s_T = (sem("c_" + a) for a in "mm rows rowsb st T".split())
            LASTC = NCOL - 1 - (NBLK - 1) * BR
            with nc.Block() as block:
                @block.sync
                def _(sp):
                    for to, of in ((dcol, dst), (scol, src)):
                        sp.dma_start(to[:, 0:NBLK - 1, :], of[EA:EA + (NBLK - 1) * BR * P].rearrange(
                            "(k r e) -> r k e", k=NBLK - 1, e=P)).then_inc(s_col, 16)
                        first = EA + (NBLK - 1) * BR * P
                        sp.dma_start(to[0:LASTC, NBLK - 1, :],
                                     of[first:first + LASTC * P].rearrange("(r e) -> r e", e=P)).then_inc(s_col, 16)
                        sp.dma_start(to[LASTC:BR, NBLK - 1, :],
                                     of[E - P:E][None, :].broadcast_to((BR - LASTC, P))).then_inc(s_col, 16)

                @block.gpsimd
                def _(pool):
                    n = [0]

                    def link(ins):
                        n[0] += 1
                        ins.then_inc(s_pool, 1)
                        pool.wait_ge(s_pool, n[0])

                    nc.gpsimd.memset(sums[0:TW, 0:2, :], 0.0)
                    nc.gpsimd.memset(which[:], 0.0)
                    nc.gpsimd.memset(within[:], 0.0)
                    link(nc.gpsimd.memset(batch[:], 1.0))
                    link(nc.gpsimd.affine_select(out=batch[:], in_=batch[:], compare_op=ALU.is_ge, fill=0.0, base=0,
                                                 pattern=[[-B, LB]], channel_multiplier=1))
                    link(nc.gpsimd.affine_select(out=batch[:], in_=batch[:], compare_op=ALU.is_ge, fill=0.0,
                                                 base=B - 1, pattern=[[B, LB]], channel_multiplier=-1))
                    for b in range(LB):
                        link(nc.gpsimd.affine_select(out=which[:], in_=which[:], compare_op=ALU.not_equal, fill=1.0,
                                                     base=-b * B, pattern=[[-1, B], [0, W]], channel_multiplier=1))
                    for p in range(B * W):
                        if p % W:
                            link(nc.gpsimd.affine_select(out=within[:], in_=within[:], compare_op=ALU.not_equal,
                                                         fill=float(p % W), base=-p, pattern=[[0, 1]],
                                                         channel_multiplier=1))

                @block.vector
                def _(v):
                    link, _ = chain(v, s_v, 0)
                    v.wait_ge(s_col, 16 * 6)
                    nc.vector.memset(ones[:], 1.0)
                    nc.vector.tensor_copy(scf[:], scol[:])
                    link(nc.vector.tensor_copy(dcf[:], dcol[:]))
                    nc.vector.tensor_reduce(cmm[:, 0, :], dcf[:], AX.X, ALU.min)
                    link(nc.vector.tensor_reduce(cmm[:, 1, :], dcf[:], AX.X, ALU.max))
                    link(nc.vector.tensor_tensor(out=cmm[:, 1, :], in0=cmm[:, 1, :], in1=cmm[:, 0, :], op=ALU.subtract))
                    v.wait_ge(s_pool, 3 + LB)
                    for k in range(NBLK):
                        last = nc.vector.tensor_scalar(starts[:, k, :], batch[:], cmm[:, 0, k:k + 1], None, ALU.mult)
                    last.then_inc(s_mm, 1)
                    v.wait_ge(s_rows_, 1)
                    for m in range(2):
                        last = nc.vector.tensor_copy(rows_mm[:, m, :], banks[m][0:1, 0:NBLK * BR])
                    last.then_inc(s_rowsb, 1)
                    v.wait_ge(s_st, 1)
                    link(nc.vector.tensor_copy(startb[:], banks[2][:, 0:NBLK * BR]))
                    link(nc.vector.tensor_reduce(bb[:], startb[:, :].rearrange("p (b c) -> p b c", c=B), AX.X, ALU.min))
                    nc.vector.tensor_copy(bbase[:], bb[0:1, :])
                    v.wait_ge(s_rowsb, 1)
                    nc.vector.tensor_reduce(bs[:], startb[0:1, :].rearrange("p (b c) -> p b c", c=B), AX.X, ALU.max)
                    link(nc.vector.tensor_reduce(bad[:, 0:1], rows_mm[:, 1, :], AX.X, ALU.max))
                    link(nc.vector.tensor_tensor(out=bs[:], in0=bs[:], in1=bb[0:1, :], op=ALU.subtract))
                    link(nc.vector.tensor_reduce(bad[:, 1:2], bs[:], AX.X, ALU.max))
                    link(nc.vector.tensor_scalar(bad[:, 0:1], bad[:, 0:1], float(W - 1), None, ALU.is_gt))
                    link(nc.vector.tensor_scalar(bad[:, 1:2], bad[:, 1:2], float(WIN - W), None, ALU.is_gt))
                    link(nc.vector.tensor_scalar(bad[:, 2:3], gspan[:], float(WIN - 1), None, ALU.is_gt))
                    link(nc.vector.tensor_reduce(bad[:, 3:4], bad[:, 0:3], AX.X, ALU.max))
                    nc.vector.tensor_copy(general[:], bad[:, 3:4])
                    v.wait_ge(s_T, 1)
                    link(nc.vector.tensor_copy(srcf[:], banks[4][:, 0:NBLK * BR]))
                    link(nc.vector.tensor_copy(srci[:], srcf[:]))
                    link(nc.vector.tensor_scalar(hii[:], srci[:], P.bit_length() - 1, None, ALU.arith_shift_right))
                    link(nc.vector.tensor_copy(hi[:], hii[:]))
                    nc.vector.scalar_tensor_tensor(out=lo[:], in0=hi[:], scalar=-float(P), in1=srcf[:], op0=ALU.mult,
                                                   op1=ALU.add)
                    link(nc.vector.tensor_tensor(out=comp[:], in0=banks[3][:, 0:NBLK * BR], in1=startb[:],
                                                 op=ALU.subtract))
                    link(nc.vector.tensor_scalar(ok[:], comp[:], float(W), None, ALU.is_lt))
                    link(nc.vector.scalar_tensor_tensor(out=comp[:], in0=hi[:], scalar=float(W), in1=comp[:],
                                                        op0=ALU.mult, op1=ALU.add))
                    link(nc.vector.scalar_tensor_tensor(out=comp[:], in0=comp[:], scalar=1.0, in1=ok[:], op0=ALU.add,
                                                        op1=ALU.mult))
                    link(nc.vector.tensor_scalar(comp[:], comp[:], -1.0, None, ALU.add))
                    if DUP:
                        link(nc.vector.memset(comp[0:DUP, NCOL - 1:NCOL], -1.0))
                    v.wait_ge(s_T, 1)
                    link(nc.vector.tensor_tensor(out=pos[0:B * W, :], in0=banks[5][0:B * W, 0:NBLK * LB],
                                                 in1=bb[0:B * W, :], op=ALU.subtract))
                    v.wait_ge(s_pool, 3 + LB + B * W - B)
                    nc.vector.tensor_scalar(pos[0:B * W, :], pos[0:B * W, :], within[0:B * W, :], None, ALU.add)

                @block.tensor
                def _(pe):
                    pe.wait_ge(s_mm, 1)
                    for m in range(2):
                        for k in range(NBLK):
                            last = nc.tensor.matmul(banks[m][0:1, k * BR:(k + 1) * BR], cmm[:, m, k:k + 1],
                                                    ident[0:BR, 0:BR], start=True, stop=True)
                    last.then_inc(s_rows_, 1)
                    for k in range(NBLK):
                        nc.tensor.matmul(banks[5][0:B * W, k * LB:(k + 1) * LB], which[:], starts[:, k, :],
                                         start=True, stop=True)
                        nc.tensor.transpose(banks[3][:, k * BR:(k + 1) * BR], dcf[:, k, :], ident[0:BR, 0:BR])
                        last = nc.tensor.transpose(banks[4][:, k * BR:(k + 1) * BR], scf[:, k, :], ident[0:BR, 0:BR])
                    last.then_inc(s_T, 1)
                    pe.wait_ge(s_rowsb, 1)
                    nc.tensor.matmul(banks[2][:, 0:NBLK * BR], ones[:], rows_mm[:, 0, :], start=True,
                                     stop=True).then_inc(s_st, 1)

        rows_of = lambda tab, i: tab[bass.ds(i * CN, CN), :].rearrange("(t p) c -> p t c", p=P)
        tiles = lambda bank, k, w: banks[bank][:, 0:k * w].rearrange("p (k c) -> p k c", c=w)

        def load_nodes(sp, to, i, s_loaded):
            sp.dma_start(to[:], rows_of(x, i)).then_inc(s_loaded, 16)

        def load_last_nodes(sp, to, s_tail, s_loaded):
            sp.dma_start(to[0:TAIL, CH - 1, :], x[N - TAIL:N, :]).then_inc(s_tail, 16)
            sp.wait_ge(s_tail, 16)
            first = (NCH - 1) * CN
            sp.dma_start(to[:, 0:CH - 1, :],
                         x[first:first + (CH - 1) * P, :].rearrange("(t p) c -> p t c", p=P)).then_inc(s_loaded, 16)

        with ExitStack() as tmp:
            xc = tmp.enter_context(nc.sbuf_tensor("n1_xc", [P, CH, C], f32))
            xT = tmp.enter_context(nc.sbuf_tensor("n1_xT", [P, CH, P], f32))
            tab = tmp.enter_context(nc.sbuf_tensor("n1_tab", [P, CH, TW], bf16))
            r = tmp.enter_context(nc.sbuf_tensor("n1_r", [P, CH, H0], f32))
            s_x, s_xt, s_xT, s_xTsb, s_p = sem("n1_x"), sem("n1_xt"), sem("n1_xT"), sem("n1_xTsb"), sem("n1_p")
            s_v, s_tab, s_st, s_kept = sem("n1_v"), sem("n1_tab"), sem("n1_st"), sem("n1_kept")
            with nc.Block() as block:
                @block.sync
                def _(sp):
                    def store(i):
                        sp.wait_ge(s_tab, i + 1)
                        sp.dma_start(rows_of(tab1, i), tab[:]).then_inc(s_st, 16)

                    @each(sp, NCH - 1)
                    def _(i):
                        need(sp, s_xT, i)
                        load_nodes(sp, xc, i, s_x)
                        store(i)
                    sp.wait_ge(s_xT, NCH - 1)
                    load_last_nodes(sp, xc, s_xt, s_x)
                    store(NCH - 1)
                    sp.wait_ge(s_st, 16 * NCH)

                @block.tensor
                def _(pe):
                    @each(pe, NCH)
                    def _(i):
                        pe.wait_ge(s_x, 16 * i + 16)
                        need(pe, s_xTsb, i)
                        for k in range(CH):
                            last = nc.tensor.transpose(banks[k // 4][:, k % 4 * P:(k % 4 + 1) * P], xc[:, k, :], ident[:])
                        last.then_inc(s_xT, 1)
                        pe.wait_ge(s_xTsb, i + 1)
                        need(pe, s_tab, i)
                        for k in range(CH):
                            last = nc.tensor.matmul(banks[2][:, k * 2 * H0:(k + 1) * 2 * H0], xT[:, k, :], WR1[:],
                                                    start=True, stop=True)
                        last.then_inc(s_p, 1)

                @block.scalar
                def _(act):
                    @each(act, NCH)
                    def _(i):
                        act.wait_ge(s_xT, i + 1)
                        need(act, s_p, i)
                        nc.scalar.copy(xT[:, 0:4, :], tiles(0, 4, P))
                        nc.scalar.copy(xT[:, 4:CH, :], tiles(1, CH - 4, P)).then_inc(s_xTsb, 1)
                        act.wait_ge(s_tab, i + 1)
                        nc.scalar.copy(table[:, bass.ds(i * CH, CH), :], tab[:]).then_inc(s_kept, 1)

                @block.vector
                def _(v):
                    nc.vector.memset(tab[:], 0.0).then_inc(s_v, 1)
                    v.wait_ge(s_v, 1)
                    nc.vector.memset(tab[:, :, ONE:ONE + 1], 1.0)
                    @each(v, NCH)
                    def _(i):
                        v.wait_ge(s_p, i + 1)
                        need(v, s_st, 16 * i)
                        need(v, s_kept, i)
                        ps = tiles(2, CH, 2 * H0)
                        nc.vector.tensor_tensor(out=xr[:, bass.ds(i * CH, CH), :], in0=ps[:, :, H0:2 * H0],
                                                in1=b1b[:, :].unsqueeze(1).broadcast_to((P, CH, H0)), op=ALU.add)
                        link, _ = chain(v, s_v, 1 + i * SPLIT)
                        split(link, tab, ps[:, :, 0:H0], r).then_inc(s_tab, 1)

        s_idx = [sem(f"a_idx{u}") for u in range(2)]
        s_rows = [sem(f"a_rows{u}") for u in range(2)]
        s_hot = sem("a_hot")
        s_sum = [sem(f"a_sum{u}") for u in range(2)]
        s_add = [sem(f"a_add{u}") for u in range(2)]
        s_ea = [sem(f"a_ea{u}") for u in range(2)]
        s_eaT, s_eaTsb, s_q, s_s = sem("a_eaT"), sem("a_eaTsb"), sem("a_q"), sem("a_s")
        s_var = [sem(f"a_var{u}") for u in range(2)]
        s_std, s_norm, s_act, s_c, s_rec = sem("a_std"), sem("a_norm"), sem("a_act"), sem("a_c"), sem("a_rec")
        of_pass = [*s_idx, s_hot, *s_sum, *s_add, *s_ea, s_eaT, s_eaTsb, s_q, s_s, *s_var, s_std,
                   s_norm, s_act, s_c, s_rec]

        def start_sums(halves, parts):
            with nc.Block() as block:
                @block.vector
                def _(v):
                    for h in halves:
                        nc.vector.memset(sums[0:parts, h, :], 0.0)
                    nc.vector.tensor_copy(rel[:], rel0[:])
                    nc.vector.tensor_copy(base[:], base0[:])

        def end_round():
            with nc.Block() as block:
                @block.gpsimd
                def _(pool):
                    pool.dma_reset(range(s_rows[0].num, s_rows[1].num + 1))
                    for s in s_rows:
                        pool.sem_clear(s)

                @block.vector
                def _(v):
                    for s in of_pass:
                        v.sem_clear(s)
                    nc.vector.tensor_scalar(rel[:], rel[:], float(WIN), None, ALU.subtract)
                    nc.vector.tensor_scalar(base[:], base[:], WIN, N, ALU.add, ALU.min)

        def load_indices(sp, i, u, last):
            need(sp, s_rows[u], 16 * G * i)
            sp.dma_start(idx[u][:], src_of(LAST if last else (2 * i + u) * GE)).then_inc(s_idx[u], 16)

        def gather(table, rows, u, w, idx, s_rows):
            nc.gpsimd.nop(nofuse=True)
            for j in range(G):
                nc.gpsimd.indirect_dma_start(
                    out=rows[u][:, j, :], out_offset=None, in_=table[:, :],
                    in_offset=bass.IndirectOffsetOnAxis(ap=idx[u][:, j:j + 1], axis=0)).then_inc(s_rows[u], 16)

        def one_hot(hot, g, u):
            for j in range(G):
                last = nc.vector.tensor_scalar(hot[u][:, j, :], iota[:], rel[:, bass.ds(g * G + j, 1)], None,
                                               ALU.is_equal)
            last.then_inc(s_hot, 1)

        def sum_pass0(table, half, rows, hot):
            with nc.Block() as block:
                @block.sync
                def _(sp):
                    @each(sp, NG // 2 - 1)
                    def _(i):
                        for u in range(2):
                            load_indices(sp, i, u, False)
                    load_indices(sp, NG // 2 - 1, 0, False)
                    load_indices(sp, NG // 2 - 1, 1, True)

                @block.gpsimd
                def _(pool):
                    @each(pool, NG // 2)
                    def _(i):
                        for u in range(2):
                            pool.wait_ge(s_idx[u], 16 * i + 16)
                            need(pool, s_sum[u], i)
                            gather(table, rows, u, TW, idx, s_rows)

                @block.vector
                def _(v):
                    @each(v, NG // 2)
                    def _(i):
                        for u in range(2):
                            need(v, s_sum[u], i)
                            one_hot(hot, 2 * i + u, u)
                        for u in range(2):
                            at = v.value_load(base[0:1, bass.ds(2 * i + u, 1)], min_val=0, max_val=N)
                            v.wait_ge(s_sum[u], i + 1)
                            need(v, s_add[1 - u], i + u)
                            to = sums[0:TW, half, bass.ds(at, WIN)]
                            nc.vector.tensor_tensor(out=to, in0=to, in1=banks[u][0:TW, 0:WIN],
                                                    op=ALU.add).then_inc(s_add[u], 1)

                @block.tensor
                def _(pe):
                    @each(pe, NG // 2)
                    def _(i):
                        for u in range(2):
                            pe.wait_ge(s_hot, 2 * i + u + 1)
                            need(pe, s_add[u], i)
                            pe.wait_ge(s_rows[u], 16 * G * i + 16 * G)
                            for j in range(G):
                                last = nc.tensor.matmul(banks[u][0:TW, 0:WIN], rows[u][:, j, :],
                                                        hot[u][:, j, :], start=j == 0, stop=j == G - 1)
                            last.then_inc(s_sum[u], 1)

        def turns_needed():
            return nc.values_load(turnsi[0:1, 0:1], min_val=1, max_val=-(-N // WIN))

        def rounds(turns, one_round):
            with nc.Fori(0, turns):
                one_round()
                end_round()

        f_oh, f_z, f_act, f_app, f_out, f_place, f_add = (
            sem("f_" + a) for a in "oh z act app out place add".split())
        f_idx = [sem(f"f_idx{u}") for u in range(4)]
        f_rows = [sem(f"f_rows{u}") for u in range(4)]
        f_hot, f_sum, f_gadd = sem("f_hot"), sem("f_sum"), sem("f_gadd")
        of_fast = [f_oh, f_z, f_act, f_app, f_out, f_place, f_add, *f_idx, f_hot, f_sum, f_gadd]
        OH = 6
        GROUP = {0: -1, 1: 0, 3: 1, 4: 2}

        def groups_before(i, q):
            return 4 * i + (-1, 0, 1, 1, 2, 3)[q]

        def fast_pass(tab_dram, half, rows, idxs, hot, lo_hot, comp_hot, counts, sumsb, place, zb):
            Z, OUT, NODE = zb, banks[6], banks[7]

            def copied(eng, t, c):
                need(eng, f_act, B * t + c + 1)

            def before(t, c, by):
                c -= by
                return (t, c) if c >= 0 else (t - 1, c + B)

            with nc.Block() as block:
                @block.sync
                def _(sp):
                    def load(g, u, k):
                        need(sp, f_rows[u], 16 * G * k)
                        sp.dma_start(idxs[u][:], src_of(g * GE)).then_inc(f_idx[u], 16)

                    @each(sp, IT)
                    def _(i):
                        for u in range(4):
                            load(4 * i + u, u, i)
                    load(4 * IT, 0, IT)

                @block.gpsimd
                def _(pool):
                    def group(g, u, k):
                        pool.wait_ge(f_idx[u], 16 * k + 16)
                        need(pool, f_sum, g - 3)
                        gather(tab_dram, rows, u, TW, idxs, f_rows)

                    @each(pool, IT)
                    def _(i):
                        for u in range(4):
                            group(4 * i + u, u, i)
                    group(4 * IT, 0, IT)

                def apply(pe, t, s, part):
                    if part == 0:
                        pe.wait_ge(f_act, B * (t + 1))
                        need(pe, f_out, t)
                    for a in range(part * NT // 7, (part + 1) * NT // 7):
                        last = nc.tensor.matmul(OUT[:, 0:TC], counts[s][:, a, :], table[:, a, 0:TC],
                                                start=a == 0, stop=a == NT - 1)
                    if part == 6:
                        last.then_inc(f_app, 1)

                def bring(pe, t, s, groups):
                    pe.wait_ge(f_out, t + 1)
                    need(pe, f_add, t)
                    need(pe, f_gadd, groups)
                    nc.tensor.matmul(NODE[0:TC, 0:WIN], sumsb[s][:], place[s][:], start=True,
                                     stop=True).then_inc(f_place, 1)

                def sum_rows(pe, g, u, k, batches):
                    pe.wait_ge(f_hot, g + 1)
                    pe.wait_ge(f_rows[u], 16 * G * k + 16 * G)
                    need(pe, f_add, batches)
                    need(pe, f_gadd, g)
                    for j in range(G):
                        last = nc.tensor.matmul(NODE[0:TC, 0:WIN], rows[u][:, j, 0:TC], hot[u % 2][:, j, :],
                                                start=j == 0, stop=j == G - 1)
                    last.then_inc(f_sum, 1)

                @block.tensor
                def _(pe):
                    @each(pe, IT)
                    def _(i):
                        for q in range(6):
                            t = 6 * i + q
                            for c in range(B):
                                n, slot, oh = B * t + c, (B * q + c) % 3, (B * q + c) % OH
                                pe.wait_ge(f_oh, n + 1)
                                if not (isinstance(n, int) and n < 3):
                                    copied(pe, *before(t, c, 3))
                                for b in range(2):
                                    last = nc.tensor.matmul(Z[slot][:, b * 512:b * 512 + HB], lo_hot[oh][:],
                                                            comp_hot[oh][:, b * HB:(b + 1) * HB], start=True,
                                                            stop=True)
                                last.then_inc(f_z, 1)
                                first = isinstance(t, int)
                                if c == 0 and (q - 1) in GROUP and not (first and t < 2):
                                    m = GROUP[q - 1]
                                    sum_rows(pe, 4 * i + m, m % 4, i if m >= 0 else i - 1, t - 2)
                                if c >= 2 and not (first and t < 1):
                                    apply(pe, t - 1, (q - 1) % 2, c - 2)
                                if c == 3 and not (first and t < 2):
                                    bring(pe, t - 2, q % 2, groups_before(i, q))
                    for part in range(7):
                        apply(pe, NB - 1, (NB - 1) % 2, part)
                    bring(pe, NB - 2, NB % 2, 4 * IT - 1)
                    sum_rows(pe, 4 * IT - 1, 3, IT - 1, NB - 1)
                    bring(pe, NB - 1, (NB - 1) % 2, 4 * IT)
                    sum_rows(pe, 4 * IT, 0, IT, NB)

                @block.scalar
                def _(act):
                    @each(act, IT)
                    def _(i):
                        for q in range(6):
                            t = 6 * i + q
                            need(act, f_app, t - 1)
                            for c in range(B):
                                act.wait_ge(f_z, B * t + c + 1)
                                to = counts[q % 2][:, :, c * W:(c + 1) * W]
                                of = Z[(B * q + c) % 3][:, :].rearrange("p (b x) -> p b x", b=2)[:, :, 0:HB]
                                nc.scalar.copy(to.rearrange("p (b a) w -> p b a w", b=2),
                                               of.rearrange("p b (a w) -> p b a w", w=W)).then_inc(f_act, 1)

                def build(v, t, q, c):
                    n, slot = B * t + c, (B * q + c) % OH
                    need(v, f_z, n - OH + 1)
                    nc.vector.tensor_scalar(lo_hot[slot][:], iota[:], lo[:, bass.ds(n, 1)], None, ALU.is_equal)
                    nc.vector.tensor_scalar(comp_hot[slot][:], wide[:], comp[:, bass.ds(n, 1)], None,
                                            ALU.is_equal).then_inc(f_oh, 1)

                def keep_sums(v, t, s):
                    v.wait_ge(f_app, t + 1)
                    need(v, f_place, t - 1)
                    nc.vector.tensor_scalar(place[s][:], iota[0:B * W, :], pos[0:B * W, bass.ds(t, 1)], None,
                                            ALU.is_equal)
                    nc.vector.tensor_copy(sumsb[s][:], OUT[0:B * W, 0:TC]).then_inc(f_out, 1)

                def add(v, start, batches, groups, done):
                    need(v, f_add, batches)
                    need(v, f_gadd, groups)
                    to = sums[0:TC, half, bass.ds(start, WIN)]
                    nc.vector.tensor_tensor(out=to, in0=to, in1=NODE[0:TC, 0:WIN], op=ALU.add).then_inc(done, 1)

                def add_batch(v, t, groups):
                    start = v.value_load(bbase[0:1, bass.ds(t, 1)], min_val=0, max_val=N)
                    v.wait_ge(f_place, t + 1)
                    add(v, start, t, groups, f_add)

                def group_hot(v, g, u, some):
                    for j in some:
                        if j == 0:
                            need(v, f_sum, g - 1)
                        last = nc.vector.tensor_scalar(hot[u % 2][:, j, :], iota[:], rel0[:, bass.ds(g * G + j, 1)],
                                                       None, ALU.is_equal)
                    if j == G - 1:
                        last.then_inc(f_hot, 1)

                def add_group(v, g, batches):
                    start = v.value_load(base0[0:1, bass.ds(g, 1)], min_val=0, max_val=N)
                    v.wait_ge(f_sum, g + 1)
                    add(v, start, batches, g, f_gadd)

                @block.vector
                def _(v):
                    @each(v, IT)
                    def _(i):
                        for q in range(6):
                            t = 6 * i + q
                            first = isinstance(t, int)
                            group = None
                            if q in GROUP and not (first and t == 0):
                                group = (4 * i + GROUP[q], GROUP[q] % 4)
                            for c in range(B):
                                build(v, t, q, c)
                                if group and c < G:
                                    group_hot(v, *group, [c])
                                if c == 2 and (q - 1) in GROUP and not (first and t < 2):
                                    add_group(v, 4 * i + GROUP[q - 1], t - 2)
                                if c == 1 and not (first and t < 2):
                                    keep_sums(v, t - 2, q % 2)
                                if c == 6 and not (first and t < 2):
                                    add_batch(v, t - 2, groups_before(i, q))
                    group_hot(v, 4 * IT - 1, 3, range(G))
                    keep_sums(v, NB - 2, NB % 2)
                    add_batch(v, NB - 2, 4 * IT - 1)
                    add_group(v, 4 * IT - 1, NB - 1)
                    keep_sums(v, NB - 1, (NB - 1) % 2)
                    add_batch(v, NB - 1, 4 * IT)
                    group_hot(v, 4 * IT, 0, range(G))
                    add_group(v, 4 * IT, NB)

        def end_fast():
            with nc.Block() as block:
                @block.gpsimd
                def _(pool):
                    pool.dma_reset(range(f_rows[0].num, f_rows[3].num + 1))
                    for s in f_rows:
                        pool.sem_clear(s)

                @block.vector
                def _(v):
                    for s in of_fast:
                        v.sem_clear(s)

        def hidden_stage():
            with ExitStack() as tmp:
                sc = tmp.enter_context(nc.sbuf_tensor("n2_sc", [TC, CN], f32))
                tab = tmp.enter_context(nc.sbuf_tensor("n2_tab", [P, CH, TW], bf16))
                r = tmp.enter_context(nc.sbuf_tensor("n2_r", [P, CH, H0], f32))
                h = tmp.enter_context(nc.sbuf_tensor("n2_h", [P, CH, H0], f32))
                inv = tmp.enter_context(nc.sbuf_tensor("n2_inv", [P, CH], f32))
                s_sc, s_m, s_v, s_tab, s_st, s_kept = (sem("n2_" + a) for a in "sc m v tab st kept".split())
                with nc.Block() as block:
                    @block.sync
                    def _(sp):
                        @each(sp, NCH)
                        def _(i):
                            sp.wait_ge(s_tab, i + 1)
                            sp.dma_start(rows_of(tab2, i), tab[:]).then_inc(s_st, 16)
                        sp.wait_ge(s_st, 16 * NCH)

                    @block.scalar
                    def _(act):
                        @each(act, NCH)
                        def _(i):
                            need(act, s_m, i)
                            nc.scalar.copy(sc[:], sums[0:TC, 0, bass.ds(i * CN, CN)]).then_inc(s_sc, 1)
                            act.wait_ge(s_tab, i + 1)
                            nc.scalar.copy(table[:, bass.ds(i * CH, CH), :], tab[:]).then_inc(s_kept, 1)

                    @block.tensor
                    def _(pe):
                        @each(pe, NCH)
                        def _(i):
                            pe.wait_ge(s_sc, i + 1)
                            need(pe, s_tab, i)
                            for k in range(CH):
                                last = nc.tensor.matmul(banks[2][:, k * 32:k * 32 + H0 + 1], sc[:, k * P:(k + 1) * P],
                                                        S[:], start=True, stop=True)
                            last.then_inc(s_m, 1)

                    @block.vector
                    def _(v):
                        nc.vector.memset(tab[:], 0.0).then_inc(s_v, 1)
                        v.wait_ge(s_v, 1)
                        nc.vector.memset(tab[:, :, ONE:ONE + 1], 1.0)
                        steps = 6 + SPLIT
                        @each(v, NCH)
                        def _(i):
                            v.wait_ge(s_m, i + 1)
                            ps = tiles(2, CH, 32)
                            at = bass.ds(i * CH, CH)

                            link, n = chain(v, s_v, 1 + i * steps)
                            nc.vector.tensor_copy(deg[:, at], ps[:, :, H0])
                            link(nc.vector.tensor_scalar(inv[:], ps[:, :, H0], 1.0, None, ALU.max))
                            link(nc.vector.reciprocal(inv[:], inv[:]))
                            nc.vector.tensor_copy(invdeg[:, at], inv[:])
                            link(nc.vector.tensor_tensor(out=h[:], in0=ps[:, :, 0:H0],
                                                         in1=inv[:, :].unsqueeze(2).broadcast_to((P, CH, H0)),
                                                         op=ALU.mult))
                            link(nc.vector.tensor_tensor(out=h[:], in0=h[:], in1=xr[:, at, :], op=ALU.add))
                            link(nc.vector.tensor_scalar(h[:], h[:], 0.0, None, ALU.max))
                            link(nc.vector.tensor_copy(hs[:, at, :], h[:]))
                            need(v, s_st, 16 * i)
                            need(v, s_kept, i)
                            split(link, tab, h[:], r).then_inc(s_tab, 1)
                            assert n[0] == steps

        def x1_stage():
            with ExitStack() as tmp:
                def t(name, shape, dt=f32):
                    return tmp.enter_context(nc.sbuf_tensor("n3_" + name, shape, dt))

                BW = QW + C + H1
                CUT = 4
                sc, xc, z = t("sc", [TC, CN]), t("xc", [P, CH, C]), t("z", [P, CH, 2 * H0])
                zT = t("zT", [2 * H0 + 1, CH, P])
                u1, st, ag = t("u", [P, CH, C]), t("st", [P, CH, 6]), t("ag", [P, CH, 2])
                std, x1c, x1T = t("std", [P, CH]), t("x1c", [P, CH, C]), t("x1T", [P, CH, P])
                tab, junk, degc = t("tab", [P, CH, RW + C]), t("junk", [P, CH, H1]), t("degc", [P, CH])
                rest, part = t("rest", [1, BW]), t("part", [1, PARTS, BW], bf16)
                bias = t("bias", [PARTS, BW], bf16)
                ones3 = t("ones3", [PARTS, P], bf16)
                s_sc, s_x, s_xt, s_m, s_z, s_zT, s_zTsb = (sem("n3_" + a) for a in "sc x xt m z zT zTsb".split())
                s_u, s_ud, s_v, s_var, s_std, s_x1, s_x1T, s_x1Tsb = (
                    sem("n3_" + a) for a in "u ud v var std x1 x1T x1Tsb".split())
                s_part, s_bias, s_wa, s_tab, s_ux, s_kept, s_split, s_st, s_deg, s_rstd = (
                    sem("n3_" + a) for a in "part bias wa tab ux kept split st deg rstd".split())
                with nc.Block() as block:
                    @block.sync
                    def _(sp):
                        def store(i):
                            sp.wait_ge(s_tab, CH * i + CUT)
                            rows = rows_of(tab3, i)
                            sp.dma_start(rows[:, 0:CUT, :], tab[:, 0:CUT, 0:RW]).then_inc(s_st, 16)
                            sp.wait_ge(s_tab, CH * i + CH)
                            sp.dma_start(rows[:, CUT:CH, :], tab[:, CUT:CH, 0:RW]).then_inc(s_st, 16)

                        load_nodes(sp, xc, 0, s_x)
                        sp.wait_ge(s_part, 1)
                        for k in range(PARTS):
                            sp.dma_start(bias[k:k + 1, :], part[:, k, :]).then_inc(s_bias, 16)
                        @each(sp, NCH - 2)
                        def _(i):
                            sp.wait_ge(s_ud, i + 1)
                            load_nodes(sp, xc, i + 1, s_x)
                            store(i)
                        sp.wait_ge(s_ud, NCH - 1)
                        load_last_nodes(sp, xc, s_xt, s_x)
                        store(NCH - 2)
                        store(NCH - 1)
                        sp.wait_ge(s_st, 32 * NCH)

                    def copy_sums(act, i):
                        need(act, s_m, i)
                        nc.scalar.copy(sc[:], sums[0:TC, 1, bass.ds(i * CN, CN)]).then_inc(s_sc, 1)

                    def copy_zT(act, i):
                        act.wait_ge(s_zT, i + 1)
                        nc.scalar.copy(zT[0:2 * H0, 0:4, :], tiles(2, 4, P)[0:2 * H0])
                        nc.scalar.copy(zT[0:2 * H0, 4:CH, :], tiles(3, CH - 4, P)[0:2 * H0]).then_inc(s_zTsb, 1)

                    def deviation(act, i):
                        act.wait_ge(s_var, i + 1)
                        nc.scalar.activation(std[:], ag[:, :, 1], ACT.Sqrt, bias=epsb[:]).then_inc(s_std, 1)

                    def keep_table(act, i, some):
                        for k in some:
                            act.wait_ge(s_wa, i * CH + k + 1)
                            nc.scalar.copy(tab[:, k, 1:RW + C], banks[4 + 2 * (k % 2)][:, 0:QW + C])
                            nc.scalar.activation(junk[:, k, :], banks[5 + 2 * (k % 2)][:, 0:H1], ACT.Square,
                                                 accum_out=tab[:, k, 0:1]).then_inc(s_tab, 1)

                    def act_step(act, i, front, sums_after):
                        act.wait_ge(s_x1T, i + 1)
                        need(act, s_wa, CH * i)
                        nc.scalar.copy(x1T[:, 0:4, :], tiles(0, 4, P))
                        nc.scalar.copy(x1T[:, 4:CH, :], tiles(1, CH - 4, P)).then_inc(s_x1Tsb, 1)
                        if front:
                            copy_zT(act, i + 1)
                        need(act, s_st, 32 * i)
                        need(act, s_ux, CH * i)
                        keep_table(act, i, range(0, 4))
                        if front:
                            deviation(act, i + 1)
                        if sums_after:
                            copy_sums(act, i + 2)
                        keep_table(act, i, range(4, CH))

                    @block.scalar
                    def _(act):
                        copy_sums(act, 0)
                        copy_zT(act, 0)
                        copy_sums(act, 1)
                        deviation(act, 0)
                        @each(act, NCH - 2)
                        def _(i):
                            act_step(act, i, True, True)
                        act_step(act, NCH - 2, True, False)
                        act_step(act, NCH - 1, False, False)

                    def sum_parts(pe, i):
                        pe.wait_ge(s_sc, i + 1)
                        need(pe, s_ud, i)
                        for k in range(CH):
                            last = nc.tensor.matmul(banks[2][:, k * H0:(k + 1) * H0], sc[:, k * P:(k + 1) * P],
                                                    S[:, 0:H0], start=True, stop=True)
                        last.then_inc(s_m, 1)

                    def turn_z(pe, i):
                        pe.wait_ge(s_z, i + 1)
                        for k in range(CH):
                            last = nc.tensor.transpose(banks[2 + k // 4][0:2 * H0, k % 4 * P:(k % 4 + 1) * P],
                                                       z[:, k, :], ident[:])
                        last.then_inc(s_zT, 1)

                    def z_products(pe, i):
                        pe.wait_ge(s_zTsb, i + 1)
                        for k in range(CH):
                            last = nc.tensor.matmul(banks[2 + k // 4][:, k % 4 * C:(k % 4 + 1) * C], zT[:, k, :],
                                                    WR2[:], start=True, stop=True)
                        last.then_inc(s_u, 1)

                    def table_products(pe, i, some):
                        for k in some:
                            if k != 1:
                                need(pe, s_tab, i * CH + max(k - 1, 0))
                            by_gamma, plain = banks[4 + 2 * (k % 2)], banks[5 + 2 * (k % 2)]
                            nc.tensor.matmul(by_gamma[:, 0:QW + C], ones3[:], bias[:, 0:QW + C], start=True, stop=False)
                            nc.tensor.matmul(by_gamma[:, 0:QW + C], x1T[:, k, :], WA[:], start=False, stop=True)
                            nc.tensor.matmul(plain[:, 0:H1], ones3[:], bias[:, QW + C:BW], start=True, stop=False)
                            nc.tensor.matmul(plain[:, 0:H1], x1T[:, k, :], WAc[:], start=False,
                                             stop=True).then_inc(s_wa, 1)

                    def pe_step(pe, i, front, sums_after):
                        pe.wait_ge(s_x1, i + 1)
                        need(pe, s_x1Tsb, i)
                        for k in range(CH):
                            last = nc.tensor.transpose(banks[k // 4][:, k % 4 * P:(k % 4 + 1) * P], x1c[:, k, :],
                                                       ident[:])
                        last.then_inc(s_x1T, 1)
                        if front:
                            turn_z(pe, i + 1)
                        pe.wait_ge(s_x1Tsb, i + 1)
                        table_products(pe, i, range(0, 1))
                        if front:
                            z_products(pe, i + 1)
                        table_products(pe, i, range(1, CH - 1))
                        if sums_after:
                            sum_parts(pe, i + 2)
                        table_products(pe, i, range(CH - 1, CH))

                    @block.tensor
                    def _(pe):
                        sum_parts(pe, 0)
                        turn_z(pe, 0)
                        z_products(pe, 0)
                        pe.wait_ge(s_bias, 16 * PARTS)
                        sum_parts(pe, 1)
                        @each(pe, NCH - 2)
                        def _(i):
                            pe_step(pe, i, True, True)
                        pe_step(pe, NCH - 2, True, False)
                        pe_step(pe, NCH - 1, False, False)

                    @block.gpsimd
                    def _(pool):
                        nc.gpsimd.memset(sums[:, 0, :], 0.0)
                        nc.gpsimd.tensor_copy(rel[:], rel0[:])
                        nc.gpsimd.tensor_copy(base[:], base0[:])
                        @each(pool, NCH)
                        def _(i):
                            pool.wait_ge(s_x1, i + 1)
                            nc.gpsimd.tensor_copy(x1s[:, bass.ds(i * CH, CH), :], x1c[:]).then_inc(s_kept, 1)
                        pool.wait_ge(s_sc, NCH)
                        nc.gpsimd.memset(sums[:, 1, :], 0.0)

                    def make_z(v, i):
                        at = bass.ds(i * CH, CH)
                        v.wait_ge(s_m, i + 1)
                        nc.vector.tensor_copy(z[:, :, H0:2 * H0], hs[:, at, :])
                        nc.vector.tensor_tensor(out=z[:, :, 0:H0], in0=tiles(2, CH, H0),
                                                in1=invdeg[:, at].unsqueeze(2).broadcast_to((P, CH, H0)),
                                                op=ALU.mult).then_inc(s_z, 1)

                    def variance(v, i):
                        link, _ = chain(v, s_v, i)
                        v.wait_ge(s_u, i + 1)
                        v.wait_ge(s_x, 16 * i + 16)
                        nc.vector.tensor_tensor(out=u1[:, 0:4, :], in0=tiles(2, 4, C), in1=xc[:, 0:4, :], op=ALU.add)
                        nc.vector.tensor_tensor(out=u1[:, 4:CH, :], in0=tiles(3, CH - 4, C),
                                                in1=xc[:, 4:CH, :], op=ALU.add).then_inc(s_ud, 1)
                        v.wait_ge(s_ud, i + 1)
                        moments(link, u1, st, ag, s_var)

                    def make_x1(v, i):
                        v.wait_ge(s_std, i + 1)
                        nc.vector.reciprocal(std[:], std[:]).then_inc(s_rstd, 1)
                        v.wait_ge(s_rstd, i + 1)
                        need(v, s_kept, i)
                        v.wait_ge(s_var, i + 1)
                        normalize(x1c, u1, ag, std).then_inc(s_x1, 1)

                    def keep_ux(v, i):
                        for k in range(CH):
                            v.wait_ge(s_tab, i * CH + k + 1)
                            nc.vector.scalar_tensor_tensor(
                                out=ux[:, bass.ds(i * CH + k, 1), :], in0=b2Wu[:, :].unsqueeze(1),
                                scalar=degc[:, k:k + 1], in1=tab[:, k, RW:RW + C].unsqueeze(1), op0=ALU.mult,
                                op1=ALU.add).then_inc(s_ux, 1)

                    def dve_step(v, i, front, sums_after):
                        need(v, s_ux, i * CH)
                        nc.vector.tensor_copy(degc[:], deg[:, bass.ds(i * CH, CH)]).then_inc(s_deg, 1)
                        if front:
                            variance(v, i + 1)
                            make_x1(v, i + 1)
                        if sums_after:
                            make_z(v, i + 2)
                        v.wait_ge(s_deg, i + 1)
                        keep_ux(v, i)

                    @block.vector
                    def _(v):
                        nc.vector.memset(zT[2 * H0:2 * H0 + 1, :, :], 1.0)
                        nc.vector.memset(ones3[:], 1.0)
                        nc.vector.tensor_copy(rest[:, 0:QW], rowA[0:1, :])
                        nc.vector.tensor_copy(rest[:, QW:QW + C], bub[0:1, :])
                        nc.vector.tensor_copy(rest[:, QW + C:BW], b1c[0:1, :]).then_inc(s_split, 1)
                        v.wait_ge(s_split, 1)
                        for k in range(PARTS - 1):
                            nc.vector.tensor_copy(part[:, k, :], rest[:]).then_inc(s_split, 1)
                            v.wait_ge(s_split, 2 * k + 2)
                            nc.vector.tensor_tensor(out=rest[:], in0=rest[:], in1=part[:, k, :],
                                                    op=ALU.subtract).then_inc(s_split, 1)
                            v.wait_ge(s_split, 2 * k + 3)
                        nc.vector.tensor_copy(part[:, PARTS - 1, :], rest[:]).then_inc(s_part, 1)
                        make_z(v, 0)
                        variance(v, 0)
                        make_x1(v, 0)
                        make_z(v, 1)
                        @each(v, NCH - 2)
                        def _(i):
                            dve_step(v, i, True, True)
                        dve_step(v, NCH - 2, True, False)
                        dve_step(v, NCH - 1, False, False)

        def moments(link, u, st, ag, s_done):
            for k in range(CH):
                last = nc.vector.bn_stats(st[:, k, :], u[:, k, :])
            link(last)
            nc.vector.nop(nofuse=True)
            for k in range(CH):
                last = nc.vector.bn_aggr(ag[:, k, :], st[:, k, :])
            last.then_inc(s_done, 1)

        def normalize(to, u, ag, rstd):
            for k in range(CH):
                last = nc.vector.tensor_scalar(to[:, k, :], u[:, k, :], ag[:, k, 0:1], rstd[:, k:k + 1],
                                               ALU.subtract, ALU.mult)
            return last

        def sum_pass1(rows, ebuf, eaT, s, hid, hot, prod, var, std, rstd):
            QB, TB, AB = range(4), 4, (5, 6)

            with nc.Block() as block:
                @block.sync
                def _(sp):
                    def load(i, u, last):
                        load_indices(sp, i, u, last)
                        need(sp, s_var[u], i)
                        sp.dma_start(ebuf[u][:], ea_of(LAST if last else (2 * i + u) * GE)).then_inc(s_ea[u], 16)

                    @each(sp, NG // 2 - 1)
                    def _(i):
                        for u in range(2):
                            load(i, u, False)
                    load(NG // 2 - 1, 0, False)
                    load(NG // 2 - 1, 1, True)

                @block.gpsimd
                def _(pool):
                    @each(pool, NG // 2)
                    def _(i):
                        for u in range(2):
                            pool.wait_ge(s_idx[u], 16 * i + 16)
                            need(pool, s_var[u], i)
                            gather(tab3, rows, u, RW, idx, s_rows)

                def turn_edges(pe, k, u):
                    g = 2 * k + u
                    pe.wait_ge(s_ea[u], 16 * k + 16)
                    need(pe, s_eaTsb, g)
                    for h in range(2):
                        last = nc.tensor.transpose(banks[TB][:, h * P:(h + 1) * P], ebuf[u][:, h * P:(h + 1) * P],
                                                   ident[:])
                    last.then_inc(s_eaT, 1)

                def products(pe, k, u):
                    g = 2 * k + u
                    pe.wait_ge(s_eaTsb, g + 1)
                    for j in range(G):
                        need(pe, s_s, G * g + j - len(QB) + 1)
                        h, q = divmod(j, P // EC)
                        nc.tensor.matmul(banks[QB[j % len(QB)]][:, 0:QW], eaT[u][q * EC:(q + 1) * EC, h, :],
                                         WQ[q * EC:(q + 1) * EC, :], start=True, stop=True).then_inc(s_q, 1)

                def sum_group(pe, k, u):
                    g = 2 * k + u
                    pe.wait_ge(s_act, 2 * g + 2)
                    pe.wait_ge(s_hot, g + 1)
                    need(pe, s_add[u], k)
                    for h in range(HH):
                        for j in range(G):
                            last = nc.tensor.matmul(banks[AB[u]][:, h * WIN:(h + 1) * WIN],
                                                    hid[u][:, j, h * P:(h + 1) * P], hot[u][:, j, :],
                                                    start=j == 0, stop=j == G - 1)
                    last.then_inc(s_sum[u], 1)

                @block.tensor
                def _(pe):
                    turn_edges(pe, 0, 0)
                    for k, u in ((0, 0), (0, 1)):
                        products(pe, k, u)
                        turn_edges(pe, k + u, 1 - u)
                    @from_one(pe, NG // 2 - 1)
                    def _(k):
                        for u in range(2):
                            products(pe, k, u)
                            turn_edges(pe, k + u, 1 - u)
                            sum_group(pe, k - 1, u)
                    k = NG // 2 - 1
                    products(pe, k, 0)
                    turn_edges(pe, k, 1)
                    sum_group(pe, k - 1, 0)
                    products(pe, k, 1)
                    sum_group(pe, k - 1, 1)
                    sum_group(pe, k, 0)
                    sum_group(pe, k, 1)

                def keep_turned(act, k, u):
                    g = 2 * k + u
                    act.wait_ge(s_eaT, g + 1)
                    nc.scalar.copy(eaT[u][:], banks[TB][:, 0:2 * P].rearrange("p (h c) -> p h c", c=P)
                                   ).then_inc(s_eaTsb, 1)

                def deviation(act, k, u):
                    act.wait_ge(s_var[u], k + 1)
                    nc.scalar.activation(std[u][:], var[u][:], ACT.Sqrt, bias=epsb[:], scale=1.0 / H1
                                         ).then_inc(s_std, 1)

                def gelu(act, k, u):
                    g = 2 * k + u
                    for b in range(2):
                        act.wait_ge(s_norm, 2 * g + b + 1)
                        part = hid[u][:, b * G // 2:(b + 1) * G // 2, :]
                        nc.scalar.activation(part, part, ACT.Gelu).then_inc(s_act, 1)

                @block.scalar
                def _(act):
                    keep_turned(act, 0, 0)
                    deviation(act, 0, 0)
                    keep_turned(act, 0, 1)
                    deviation(act, 0, 1)
                    keep_turned(act, 1, 0)
                    gelu(act, 0, 0)
                    with act.Fori(1, NG // 2 - 1) as k:
                        for u in range(2):
                            deviation(act, k, u)
                            keep_turned(act, k + u, 1 - u)
                            gelu(act, k - 1 + u, 1 - u)
                    k = NG // 2 - 1
                    deviation(act, k, 0)
                    keep_turned(act, k, 1)
                    gelu(act, k - 1, 1)
                    deviation(act, k, 1)
                    gelu(act, k, 0)
                    gelu(act, k, 1)

                def add_rows(v, k, u):
                    g = 2 * k + u
                    need(v, s_norm, 2 * g - 2)
                    v.wait_ge(s_rows[u], 16 * G * k + 16 * G)
                    for j in range(G):
                        v.wait_ge(s_q, G * g + j + 1)
                        nc.vector.tensor_tensor(out=s[u][:, j, :], in0=rows[u][:, j, 1:RW],
                                                in1=banks[QB[j % len(QB)]][:, 0:QW], op=ALU.add).then_inc(s_s, 1)
                    v.wait_ge(s_s, G * g + G)
                    v.wait_ge(s_ea[u], 16 * k + 16)
                    link, _ = chain(v, s_c, 3 * g)
                    link(nc.vector.tensor_tensor(out=prod[:], in0=s[u][:, :, H1:QW],
                                                 in1=ebuf[u][:, :].rearrange("p (j c) -> p j c", c=EC), op=ALU.mult))
                    link(nc.vector.tensor_reduce(var[u][:], prod[:], AX.X, ALU.add))
                    link(nc.vector.tensor_tensor(out=var[u][:], in0=var[u][:], in1=rows[u][:, :, 0], op=ALU.add))
                    nc.vector.tensor_scalar(var[u][:], var[u][:], 0.0, None, ALU.max).then_inc(s_var[u], 1)

                def scale_rows(v, k, u):
                    g = 2 * k + u
                    v.wait_ge(s_std, g + 1)
                    need(v, s_norm, 2 * g)
                    nc.vector.reciprocal(rstd[:], std[u][:]).then_inc(s_rec, 1)
                    v.wait_ge(s_rec, g + 1)
                    for j in range(G):
                        last = nc.vector.scalar_tensor_tensor(out=hid[u][:, j, :], in0=s[u][:, j, 0:H1],
                                                              scalar=rstd[:, j:j + 1], in1=be1b[:], op0=ALU.mult,
                                                              op1=ALU.add)
                        if j % 4 == 3:
                            last.then_inc(s_norm, 1)
                    one_hot(hot, g, u)

                def add_sums(v, k, u):
                    g = 2 * k + u
                    at = v.value_load(base[0:1, bass.ds(g, 1)], min_val=0, max_val=N)
                    v.wait_ge(s_sum[u], k + 1)
                    need(v, s_add[1 - u], k + u)
                    to = sums[:, :, bass.ds(at, WIN)]
                    nc.vector.tensor_tensor(out=to, in0=to, in1=banks[AB[u]][:, 0:HH * WIN].rearrange(
                        "p (h n) -> p h n", h=HH), op=ALU.add).then_inc(s_add[u], 1)

                @block.vector
                def _(v):
                    add_rows(v, 0, 0)
                    add_rows(v, 0, 1)
                    scale_rows(v, 0, 0)
                    @from_one(v, NG // 2)
                    def _(k):
                        for u in range(2):
                            add_rows(v, k, u)
                            scale_rows(v, k - 1 + u, 1 - u)
                            add_sums(v, k - 1, u)
                    k = NG // 2 - 1
                    scale_rows(v, k, 1)
                    add_sums(v, k, 0)
                    add_sums(v, k, 1)

        def update_stage():
            with ExitStack() as tmp:
                def t(name, shape, dt=f32):
                    return tmp.enter_context(nc.sbuf_tensor("n4_" + name, shape, dt))

                sc = t("sc", [P, HH, CN])
                u1, w, y = t("u", [P, CH, C]), t("w", [P, CH, C]), t("y", [P, CH, C])
                st, ag, std = t("st", [P, CH, 6]), t("ag", [P, CH, 2]), t("std", [P, CH])
                s_sc, s_m, s_v, s_var, s_std, s_g, s_gd, s_y, s_st, s_stt = (
                    sem("n4_" + a) for a in "sc m v var std g gd y st stt".split())
                with nc.Block() as block:
                    @block.sync
                    def _(sp):
                        @each(sp, NCH - 1)
                        def _(i):
                            sp.wait_ge(s_y, i + 1)
                            sp.dma_start(rows_of(out, i), y[:]).then_inc(s_st, 16)
                        sp.wait_ge(s_y, NCH)
                        first = (NCH - 1) * CN
                        sp.dma_start(out[first:first + (CH - 1) * P, :].rearrange("(t p) c -> p t c", p=P),
                                     y[:, 0:CH - 1, :]).then_inc(s_st, 16)
                        sp.dma_start(out[N - TAIL:N, :], y[0:TAIL, CH - 1, :]).then_inc(s_stt, 16)
                        sp.wait_ge(s_st, 16 * NCH)
                        sp.wait_ge(s_stt, 16)

                    @block.scalar
                    def _(act):
                        @each(act, NCH)
                        def _(i):
                            need(act, s_m, i)
                            nc.scalar.copy(sc[:], sums[:, :, bass.ds(i * CN, CN)]).then_inc(s_sc, 1)
                            for n in range(2):
                                act.wait_ge(s_var, 2 * i + n + 1)
                                nc.scalar.activation(std[:], ag[:, :, 1], ACT.Sqrt, bias=epsb[:]).then_inc(s_std, 1)
                                if n == 0:
                                    act.wait_ge(s_g, i + 1)
                                    nc.scalar.activation(w[:], w[:], ACT.Gelu).then_inc(s_gd, 1)

                    @block.tensor
                    def _(pe):
                        @each(pe, NCH)
                        def _(i):
                            pe.wait_ge(s_sc, i + 1)
                            need(pe, s_y, i)
                            for k in range(CH):
                                for h in range(HH):
                                    last = nc.tensor.matmul(banks[k // 4][:, k % 4 * C:(k % 4 + 1) * C],
                                                            sc[:, h, k * P:(k + 1) * P], W2Wu[:, h, :],
                                                            start=h == 0, stop=h == HH - 1)
                            last.then_inc(s_m, 1)

                    @block.vector
                    def _(v):
                        steps = 9
                        @each(v, NCH)
                        def _(i):
                            link, n = chain(v, s_v, i * steps)
                            v.wait_ge(s_m, i + 1)
                            nc.vector.tensor_tensor(out=u1[:, 0:4, :], in0=tiles(0, 4, C),
                                                    in1=ux[:, bass.ds(i * CH, 4), :], op=ALU.add)
                            link(nc.vector.tensor_tensor(out=u1[:, 4:CH, :], in0=tiles(1, CH - 4, C),
                                                         in1=ux[:, bass.ds(i * CH + 4, CH - 4), :], op=ALU.add))
                            moments(link, u1, st, ag, s_var)
                            v.wait_ge(s_std, 2 * i + 1)
                            link(nc.vector.reciprocal(std[:], std[:]))
                            link(normalize(w, u1, ag, std))
                            link(nc.vector.tensor_tensor(out=w[:], in0=w[:], op=ALU.mult,
                                                         in1=gub[:, :].unsqueeze(1).broadcast_to((P, CH, C))))
                            nc.vector.tensor_tensor(out=w[:], in0=w[:], in1=beub[:, :].unsqueeze(1).broadcast_to(
                                (P, CH, C)), op=ALU.add).then_inc(s_g, 1)
                            link(nc.vector.tensor_scalar(u1[:], x1s[:, bass.ds(i * CH, CH), :], 2.0, None, ALU.mult))
                            v.wait_ge(s_gd, i + 1)
                            link(nc.vector.tensor_tensor(out=u1[:], in0=u1[:], in1=w[:], op=ALU.add))
                            moments(link, u1, st, ag, s_var)
                            v.wait_ge(s_std, 2 * i + 2)
                            link(nc.vector.reciprocal(std[:], std[:]))
                            need(v, s_st, 16 * i)
                            normalize(y, u1, ag, std).then_inc(s_y, 1)
                            assert n[0] == steps, n

        with ExitStack() as tmp:
            def some(n, name, shape, dt=f32):
                return [tmp.enter_context(nc.sbuf_tensor(f"{name}{u}", shape, dt)) for u in range(n)]

            rows, idxs = some(4, "rows0_", [P, G, TW], bf16), some(4, "idx0_", [P, G], i32)
            hot, lo_hot, comp_hot = (some(2, "hot0_", [P, G, WIN], bf16), some(OH, "lo_hot", [P, P], bf16),
                                     some(OH, "comp_hot", [P, 2 * HB], bf16))
            counts = some(2, "counts", [P, HI, P], bf16)
            sumsb, place = some(2, "sumsb", [B * W, TC]), some(2, "place", [B * W, WIN])

            def sum_edges(tab_dram, half):
                fast_pass(tab_dram, half, rows, idxs, hot, lo_hot, comp_hot, counts, sumsb, place, zbanks)
                end_fast()
                with nc.If(nc.values_load(general[0:1, 0:1], min_val=0, max_val=1)):
                    turns = turns_needed()
                    start_sums((half,), TW)
                    rounds(turns, lambda: sum_pass0(tab_dram, half, rows, hot))
                nc.end_all_ifs()

            with nc.Block() as block:
                @block.vector
                def _(v):
                    for s in range(2):
                        nc.vector.memset(counts[s][:, :, B * W:P], 0.0)

            sum_edges(tab1, 0)
            hidden_stage()
            sum_edges(tab2, 1)
        x1_stage()
        with ExitStack() as tmp:
            def two(name, shape, dt=f32):
                return [tmp.enter_context(nc.sbuf_tensor(f"{name}{u}", shape, dt)) for u in range(2)]

            rows, ebuf, eaT = two("rows1_", [P, G, RW]), two("ebuf", [P, G * EC]), two("eaT", [P, 2, P])
            s, hid, hot = two("s", [P, G, QW]), two("hid", [P, G, H1]), two("hot1_", [P, G, WIN])
            var, std = two("var", [P, G]), two("std", [P, G])
            prod = tmp.enter_context(nc.sbuf_tensor("prod", [P, G, EC], f32))
            rstd = tmp.enter_context(nc.sbuf_tensor("rstd", [P, G], f32))
            rounds(turns_needed(), lambda: sum_pass1(rows, ebuf, eaT, s, hid, hot, prod, var, std, rstd))
        update_stage()


_INS = ['x', 'src', 'dst', 'edge_attr_32', 'L0_gnn_W1', 'L0_gnn_b1', 'L0_gnn_R1', 'L0_gnn_W2', 'L0_gnn_b2', 'L0_gnn_R2',
        'L1_gnn_W1', 'L1_gnn_b1', 'L1_gnn_g1', 'L1_gnn_be1', 'L1_gnn_W2', 'L1_gnn_b2', 'L1_gnn_Wu', 'L1_gnn_bu',
        'L1_gnn_gu', 'L1_gnn_beu']


def kernel(**inputs):
    import numpy as _np
    import concourse.bacc as _bacc
    from concourse import mybir as _mybir
    from concourse.bass_utils import run_bass_kernel_spmd as _run

    nc = _bacc.Bacc("TRN2", target_bir_lowering=False, num_devices=1)
    arrays, args = {}, {}
    for name in _INS:
        a = _np.ascontiguousarray(inputs[name])
        arrays[f"in_{name}"] = a
        args[name] = nc.dram_tensor(f"in_{name}", a.shape, _mybir.dt.from_np(a.dtype), kind="ExternalInput").ap()
    out = nc.dram_tensor("out", args["x"].shape, _mybir.dt.float32, kind="ExternalOutput").ap()
    weights = {name.replace("_gnn", ""): args[name] for name in _INS[4:]}
    gnn(nc, args["x"], args["src"], args["dst"], args["edge_attr_32"], weights, out)
    r = _run(nc, [arrays], core_ids=[0])
    return r.results[0]["out"]
```
